# Optimizing a Trainium2 kernel written in Bass

```python
import numpy as np
import jax
import jax.numpy as jnp

def _softmax(x, axis=-1):
    return jax.nn.softmax(x, axis=axis)

def _gelu(x):
    return jax.nn.gelu(x, approximate=True)

def _silu(x):
    return jax.nn.silu(x)

def _sigmoid(x):
    return jax.nn.sigmoid(x)

def _layernorm(x, axis=-1, eps=1e-05):
    m = jnp.mean(x, axis=axis, keepdims=True)
    v = jnp.var(x, axis=axis, keepdims=True)
    return (x - m) / jnp.sqrt(v + eps)

def _scatter_add(tgt, idx, src, axis=0):
    return tgt.at[idx].add(src)

def _segment_sum(src, seg, n):
    return jax.ops.segment_sum(src, seg, n)
kernel_name = 'mk_cond_resid_d4_seqx_r8_cb097a'

def setup_inputs(seed: int=0):
    np.random.seed(seed)
    _w = jnp.asarray

    def _rec_inputs():
        import jax
        import jax.numpy as jnp
        _rk = jax.random.key(seed)
        x = -7.109e-05 + 0.9999 * jax.random.normal(jax.random.fold_in(_rk, 1), (128, 32, 512), jnp.float32)
        _lenS = 32 - jax.random.randint(jax.random.fold_in(_rk, 7), (128,), 0, max(1, 32 // 4) + 1, jnp.int32)
        _lenS2 = 32 - jax.random.randint(jax.random.fold_in(_rk, 8), (128,), 0, max(1, 32 // 4) + 1, jnp.int32)
        itok_B_0_15 = jax.random.randint(jax.random.fold_in(_rk, 11), (128,), 0, 16, jnp.int32)
        itok_B_3_7 = jax.random.randint(jax.random.fold_in(_rk, 12), (128,), 3, 8, jnp.int32)
        itok_B_2_6 = jax.random.randint(jax.random.fold_in(_rk, 13), (128,), 2, 7, jnp.int32)
        itok_B_0_7 = jax.random.randint(jax.random.fold_in(_rk, 14), (128,), 0, 8, jnp.int32)
        itok_B_2182_4065 = jax.random.randint(jax.random.fold_in(_rk, 16), (128,), 2182, 4066, jnp.int32)
        return (x, itok_B_0_15, itok_B_3_7, itok_B_2_6, itok_B_0_7, itok_B_2182_4065, _lenS)
    x, itok_B_0_15, itok_B_3_7, itok_B_2_6, itok_B_0_7, itok_B_2182_4065, _lenS = _rec_inputs()

    def _L0_cond_setup():
        import jax, jax.numpy as jnp
        import numpy as np
        NUM_CONDITIONS = 16
        IN_CH = 32
        OUT_CH = 32
        B = 64
        T = 512
        key = jax.random.key(seed)
        k_x, k_w, k_c = jax.random.split(key, 3)
        x = jax.random.normal(k_x, (B, IN_CH, T), dtype=jnp.float32)
        bound = float(np.sqrt(6.0 / IN_CH))
        weights = jax.random.uniform(k_w, (NUM_CONDITIONS, IN_CH, OUT_CH), dtype=jnp.float32, minval=-bound, maxval=bound)
        condition = jax.random.randint(k_c, (B,), 0, NUM_CONDITIONS, dtype=jnp.int64)
        return {'x': x, 'weights': weights, 'condition': condition}
    _L0_cond_all = _L0_cond_setup()
    _L0_cond_in = {k: v for k, v in _L0_cond_all.items() if k in ('weights',)}
    del _L0_cond_all

    def _L1_cond_setup():
        import jax, jax.numpy as jnp
        import numpy as np
        RANK = 16
        ALPHA = 16.0
        SCALING = ALPHA / RANK
        N_ADAPTERS = 8
        IN_F = 512
        OUT_F = 512
        BATCH = 4
        SEQ = 256
        key = jax.random.key(seed)
        kx, ka, kb, ki = jax.random.split(key, 4)
        x = jax.random.normal(kx, (BATCH, SEQ, IN_F), dtype=jnp.float32)
        A = jax.random.normal(ka, (N_ADAPTERS, OUT_F, RANK), dtype=jnp.float32) * 0.02
        B = jax.random.normal(kb, (N_ADAPTERS, RANK, IN_F), dtype=jnp.float32) * 0.02
        adapter_ids = jax.random.randint(ki, (BATCH,), 0, N_ADAPTERS, dtype=jnp.int32)
        return {'x': x, 'A': A, 'B': B, 'adapter_ids': adapter_ids}
    _L1_cond_all = _L1_cond_setup()
    _L1_cond_in = {k: v for k, v in _L1_cond_all.items() if k in ('A', 'B')}
    del _L1_cond_all

    def _L2_cond_setup():
        import jax, jax.numpy as jnp
        import numpy as np
        B, N, H, F = (4, 64, 512, 1376)
        L, R, RANK = (1, 16, 16)
        SCALE = 0.5
        key = jax.random.key(seed)
        ks = jax.random.split(key, 12)
        nrm = lambda k, shape, fan: jax.random.normal(k, shape, jnp.float32) * fan ** (-0.5)
        inp = {'x': jax.random.normal(ks[0], (B, N, H), jnp.float32), 'W_gate': nrm(ks[1], (F, H), H), 'W_up': nrm(ks[2], (F, H), H), 'W_down': nrm(ks[3], (H, F), F), 'A_gate': nrm(ks[4], (L, R, RANK, H), H), 'B_gate': nrm(ks[5], (L, R, F, RANK), RANK), 'A_up': nrm(ks[6], (L, R, RANK, H), H), 'B_up': nrm(ks[7], (L, R, F, RANK), RANK), 'A_down': nrm(ks[8], (L, R, RANK, F), F), 'B_down': nrm(ks[9], (L, R, H, RANK), RANK), 'lora_indices': jax.random.randint(ks[10], (B,), 0, R), 'layer_idx': 0}
        return inp
    _L2_cond_all = _L2_cond_setup()
    _L2_cond_in = {k: v for k, v in _L2_cond_all.items() if k in ('W_gate', 'W_up', 'W_down', 'A_gate', 'B_gate', 'A_up', 'B_up', 'A_down', 'B_down')}
    del _L2_cond_all

    def _L3_cond_setup():
        import jax, jax.numpy as jnp
        import numpy as np
        SESSION_CHANNELS = [128, 160, 192, 224, 240, 248, 252, 32]
        N_SESS = len(SESSION_CHANNELS)
        B, MAX_C, MAX_T = (16, 32, 512)
        HID, N_SRC = (64, 32)
        key = jax.random.key(seed)
        ks = jax.random.split(key, 7)
        session_ids = jax.random.randint(ks[0], (B,), 0, N_SESS)
        chan_table = jnp.asarray(SESSION_CHANNELS)
        channel_counts = chan_table[session_ids]
        seq_lens = jax.random.randint(ks[1], (B,), MAX_T // 2, MAX_T + 1)
        x = jax.random.normal(ks[2], (B, MAX_C, MAX_T), jnp.float32)
        cmask = (jnp.arange(MAX_C)[None, :] < channel_counts[:, None]).astype(x.dtype)
        tmask = (jnp.arange(MAX_T)[None, :] < seq_lens[:, None]).astype(x.dtype)
        x = x * cmask[:, :, None] * tmask[:, None, :]
        lim1 = 1.0 / np.sqrt(MAX_C)
        W_sess = jax.random.uniform(ks[3], (N_SESS, MAX_C, HID), jnp.float32, -lim1, lim1)
        b_sess = jax.random.uniform(ks[4], (N_SESS, HID), jnp.float32, -lim1, lim1)
        lim2 = 1.0 / np.sqrt(HID)
        W2 = jax.random.uniform(ks[5], (HID, N_SRC), jnp.float32, -lim2, lim2)
        b2 = jax.random.uniform(ks[6], (N_SRC,), jnp.float32, -lim2, lim2)
        return dict(x=x, session_ids=session_ids, channel_counts=channel_counts, seq_lens=seq_lens, W_sess=W_sess, b_sess=b_sess, W2=W2, b2=b2)
    _L3_cond_all = _L3_cond_setup()
    _L3_cond_in = {k: v for k, v in _L3_cond_all.items() if k in ('W_sess', 'b_sess', 'W2', 'b2')}
    del _L3_cond_all
    return {'x': x, 'itok_B_0_15': itok_B_0_15, 'itok_B_3_7': itok_B_3_7, 'itok_B_2_6': itok_B_2_6, 'itok_B_0_7': itok_B_0_7, 'itok_B_2182_4065': itok_B_2182_4065, '_lenS': _lenS, 'L0_cond_weights': _L0_cond_in['weights'], 'L1_cond_A': _L1_cond_in['A'], 'L1_cond_B': _L1_cond_in['B'], 'L2_cond_W_gate': _L2_cond_in['W_gate'], 'L2_cond_W_up': _L2_cond_in['W_up'], 'L2_cond_W_down': _L2_cond_in['W_down'], 'L2_cond_A_gate': _L2_cond_in['A_gate'], 'L2_cond_B_gate': _L2_cond_in['B_gate'], 'L2_cond_A_up': _L2_cond_in['A_up'], 'L2_cond_B_up': _L2_cond_in['B_up'], 'L2_cond_A_down': _L2_cond_in['A_down'], 'L2_cond_B_down': _L2_cond_in['B_down'], 'L3_cond_W_sess': _L3_cond_in['W_sess'], 'L3_cond_b_sess': _L3_cond_in['b_sess'], 'L3_cond_W2': _L3_cond_in['W2'], 'L3_cond_b2': _L3_cond_in['b2']}

def reference(x, itok_B_0_15, itok_B_3_7, itok_B_2_6, itok_B_0_7, itok_B_2182_4065, _lenS, L0_cond_weights, L1_cond_A, L1_cond_B, L2_cond_W_gate, L2_cond_W_up, L2_cond_W_down, L2_cond_A_gate, L2_cond_B_gate, L2_cond_A_up, L2_cond_B_up, L2_cond_A_down, L2_cond_B_down, L3_cond_W_sess, L3_cond_b_sess, L3_cond_W2, L3_cond_b2):
    import jax
    import jax.numpy as jnp

    def _L0_cond_ref(x, weights, condition):
        import jax, jax.numpy as jnp
        import numpy as np
        NUM_CONDITIONS = 16
        IN_CH = 32
        OUT_CH = 32
        B = 64
        T = 512
        W = weights[condition]
        return jnp.einsum('bct,bcd->bdt', x, W)

    def _L1_cond_ref(x, A, B, adapter_ids):
        import jax, jax.numpy as jnp
        import numpy as np
        RANK = 16
        ALPHA = 16.0
        SCALING = ALPHA / RANK
        N_ADAPTERS = 8
        IN_F = 512
        OUT_F = 512
        BATCH = 4
        SEQ = 256
        B_sel = B[adapter_ids]
        A_sel = A[adapter_ids]
        Bx = jnp.einsum('bni,bri->bnr', x, B_sel)
        out = jnp.einsum('bnr,bor->bno', Bx, A_sel)
        return out * SCALING

    def _L2_cond_ref(x, W_gate, W_up, W_down, A_gate, B_gate, A_up, B_up, A_down, B_down, lora_indices, layer_idx):
        import jax, jax.numpy as jnp
        import numpy as np
        B, N, H, F = (4, 64, 512, 1376)
        L, R, RANK = (1, 16, 16)
        SCALE = 0.5

        def lora_add(base, inp, A, B):
            Ab = A[layer_idx][lora_indices]
            Bb = B[layer_idx][lora_indices]
            t = jnp.einsum('bri,bni->bnr', Ab, inp)
            return base + jnp.einsum('bor,bnr->bno', Bb, t) * SCALE
        gate = lora_add(jnp.einsum('bnh,fh->bnf', x, W_gate), x, A_gate, B_gate)
        up = lora_add(jnp.einsum('bnh,fh->bnf', x, W_up), x, A_up, B_up)
        act = jax.nn.silu(gate) * up
        down = lora_add(jnp.einsum('bnf,hf->bnh', act, W_down), act, A_down, B_down)
        return down

    def _L3_cond_ref(x, session_ids, channel_counts, seq_lens, W_sess, b_sess, W2, b2):
        import jax, jax.numpy as jnp
        import numpy as np
        SESSION_CHANNELS = [128, 160, 192, 224, 240, 248, 252, 32]
        N_SESS = len(SESSION_CHANNELS)
        B, MAX_C, MAX_T = (16, 32, 512)
        HID, N_SRC = (64, 32)
        cmask = (jnp.arange(x.shape[1])[None, :] < channel_counts[:, None]).astype(x.dtype)
        xm = x * cmask[:, :, None]
        W = W_sess[session_ids]
        b = b_sess[session_ids]
        h = jnp.einsum('bct,bch->bht', xm, W) + b[:, :, None]
        h = jax.nn.gelu(h, approximate=False)
        out = jnp.einsum('bht,hs->bst', h, W2) + b2[None, :, None]
        tmask = (jnp.arange(x.shape[2])[None, :] < seq_lens[:, None]).astype(x.dtype)
        return out * tmask[:, None, :]
    x = x + _L0_cond_ref(x, L0_cond_weights, itok_B_0_15)
    x = x + _L1_cond_ref(x, L1_cond_A, L1_cond_B, itok_B_3_7)
    x = x + _L2_cond_ref(x, L2_cond_W_gate, L2_cond_W_up, L2_cond_W_down, L2_cond_A_gate, L2_cond_B_gate, L2_cond_A_up, L2_cond_B_up, L2_cond_A_down, L2_cond_B_down, itok_B_2_6, 0)
    x = x + _L3_cond_ref(x, itok_B_0_7, _lenS, itok_B_2182_4065, L3_cond_W_sess, L3_cond_b_sess, L3_cond_W2, L3_cond_b2)
    return x

_drawn_inputs = setup_inputs


def setup_inputs(seed=0):
    import zlib

    import numpy as np

    out = dict(_drawn_inputs(seed))
    spreads = {}
    factors = {'L3_cond_b_sess': 4.988}
    for name, (base, spread) in spreads.items():
        noise = np.random.default_rng([zlib.crc32(name.encode()), seed]).standard_normal(out[name].shape)
        drawn = base * np.exp(spread * noise) if base else spread * noise
        out[name] = jnp.asarray(drawn.astype(out[name].dtype))
    for name, factor in factors.items():
        out[name] = (out[name] * factor).astype(out[name].dtype)
    return out
```

```python
BATCH, CH, T = 128, 32, 512
P = 128
NBG = P // CH
G = BATCH // NBG
KH = T // P
F = 1376
FC = -(-F // P)
FLAST = F - (FC - 1) * P
RK = 16
NA1, NA2, NS = 8, 16, 8
HID = 64
BLOCKS = [(0, 512), (512, 512), (1024, F - 1024)]
BROW = 2 * F + T
AGU, AGD = 2 * KH * RK, FC * RK
FQ = 16
FP = F // FQ


def build(nc, bass, mybir, x, c0, c1, c2, c3, seqlen, chans, W0, A1, B1, Wg, Wu, Wd, Ag, Bg, Au, Bu,
          Ad, Bd, W3, b3, W2, b2, out):
    from contextlib import ExitStack

    F32, R32, I32, I16 = mybir.dt.float32, mybir.dt.float32r, mybir.dt.int32, mybir.dt.int16
    ALU, ACT = mybir.AluOpType, mybir.ActivationFunctionType
    ctx = ExitStack()
    with ctx:
        ctx.enter_context(nc.allow_non_contiguous_dma(reason="small tables, once"))

        def sb(name, shape, dt):
            return ctx.enter_context(nc.sbuf_tensor(name, shape, dt))

        def sem(name):
            return ctx.enter_context(nc.semaphore(name))

        def f(ap):
            return ap.bitcast(F32)

        ident = sb("ident", [P, P], F32)
        ident_r = sb("ident_r", [P, P], R32)
        mask = sb("mask", [P, P], F32)
        both = sb("both", [P, P], F32)
        pidx = sb("pidx", [P, 4], I32)
        colf = sb("colf", [P, 4], F32)
        iota_t = sb("iota_t", [P, T], I16)
        meta = sb("meta", [P, G, 4], F32)
        cols = sb("cols", [P, 4], F32)
        b2col = sb("b2col", [P, 1], F32)
        idx = sb("idx", [4, BATCH], I32)
        w0raw = sb("w0raw", [P, P], F32)
        w0i = sb("w0i", [P, P], F32)
        w0h, w0l = sb("w0h", [P, P], R32), sb("w0l", [P, P], R32)
        w3raw = sb("w3raw", [P, NBG * HID], F32)
        w3h, w3l = sb("w3h", [P, NBG * HID], R32), sb("w3l", [P, NBG * HID], R32)
        w2raw = sb("w2raw", [P, 192], F32)
        w2h, w2l = sb("w2h", [P, 192], R32), sb("w2l", [P, 192], R32)

        at_w = nc.sbuf_base
        wguh, wgul = (sb(n, [P, KH, 2 * F], R32) for n in ("wguh", "wgul"))
        wdh, wdl = (sb(n, [P, FC, T], R32) for n in ("wdh", "wdl"))

        at_work = nc.sbuf_base
        xraw = sb("xraw", [P, T], F32)
        xsh, xsl = sb("xsh", [P, T], R32), sb("xsl", [P, T], R32)
        x2h, x2l = sb("x2h", [P, T], R32), sb("x2l", [P, T], R32)
        x3raw = sb("x3raw", [P, T], F32)
        ag1r, ag1 = sb("ag1r", [P, NBG, KH * RK], F32), sb("ag1", [P, KH, P], R32)
        agur, agu = sb("agur", [P, NBG, AGU], F32), sb("agu", [P, 2 * KH, P], R32)
        agdr, agd = sb("agdr", [P, NBG, AGD], F32), sb("agd", [P, FC, P], R32)
        bg1 = sb("bg1", [P, T], F32)
        bgu = sb("bgu", [P, 2 * F], F32)
        bgd = sb("bgd", [P, T], F32)
        ringh, ringl = (sb(n, [P, 2, 512], R32) for n in ("ringh", "ringl"))
        tma, tmb = sb("tma", [P, P], F32), sb("tmb", [P, P], F32)
        tm = {"t1": tma, "td": tmb, "tg": tma, "tu": tmb}
        tms = sb("tms", [P, P], F32)
        hh = sb("hh", [P, P], R32)
        ts = {c: sb(f"ts_{c}", [P, P], R32) for c in ("t1", "tg", "tu", "td")}
        sil, act_ = sb("sil", [P, 512], F32), sb("act_", [P, 512], F32)
        ath, atl = (sb(n, [P, 2, 512], R32) for n in ("ath", "atl"))
        graw = sb("graw", [P, 2, T], F32)
        gh, gl = (sb(n, [P, 2, T], R32) for n in ("gh", "gl"))
        x1h, x1l = gh[:, 1, :], gl[:, 1, :]

        def at(place):
            here = [place]

            def alloc(name, shape, dt):
                n = 4
                for s in shape[1:]:
                    n *= s
                t = nc.alloc_sbuf_tensor_at(name, shape, dt, offset=here[0])
                here[0] += -(-n // 32) * 32
                return t
            return alloc

        st = at(at_w)
        nbg, nbu = (st(n, [FP, NA2, FQ * RK], F32) for n in ("nbg", "nbu"))
        nbd = st("nbd", [P, NA2, KH * RK], F32)
        nb1 = st("nb1", [P, NA1, KH * RK], F32)
        rows2 = st("rows2", [P, 2, BROW], F32)
        rows1 = st("rows1", [P, T], F32)
        nag, nau = (st(n, [P, 2, T], F32) for n in ("nag", "nau"))
        nad = st("nad", [P, 2, F], F32)
        na1 = st("na1", [P, T], F32)
        tab2 = st("tab2", [P, NA2, AGU + AGD], F32)
        tab1 = st("tab1", [P, NA1, KH * RK], F32)
        pbg = st("pbg", [FP, FQ, NA2, RK], F32)
        bci, bcc, bcs = (st(n, [P, BATCH], I32) for n in ("bci", "bcc", "bcs"))
        b3t = st("b3t", [P, NS], F32)
        btmp = st("btmp", [P, G, 2], F32)
        st = at(at_work)
        nwg, nwu = (st(n, [P, FC, T], F32) for n in ("nwg", "nwu"))
        pbu = st("pbu", [FP, FQ, NA2, RK], F32)
        pbd = st("pbd", [P, KH, NA2, RK], F32)
        pb1 = st("pb1", [P, KH, NA1, RK], F32)
        nwd = at(at_work)("nwd", [P, KH, F], F32)

        scr_a1 = nc.dram_tensor("scr_a1", [NA1, P, KH * RK], F32, kind="Internal").ap()
        scr_a2 = nc.dram_tensor("scr_a2", [NA2, P, AGU + AGD], F32, kind="Internal").ap()
        scr_b1 = nc.dram_tensor("scr_b1", [NA1, 2, RK, T], F32, kind="Internal").ap()
        scr_b2 = nc.dram_tensor("scr_b2", [NA2, 2, RK, BROW], F32, kind="Internal").ap()

        bank = [ctx.enter_context(nc.psum_tensor(f"bank{i}", [P, 512], F32)) for i in range(8)]
        GATE = [bank[0], bank[2], bank[0]]
        UP = [bank[1], bank[3], bank[1]]
        X, TP, D, M = bank[4], bank[5], bank[6], bank[7]
        HB = [D, TP]

        d_small, d_bn, d_an, d_wn = sem("d_small"), sem("d_bn"), sem("d_an"), sem("d_wn")
        d_scr = sem("d_scr")
        d_x, d_w0, d_ag1, d_bg1, d_agu = (sem(f"d_{n}") for n in ("x", "w0", "ag1", "bg1", "agu"))
        d_bgu, d_agd, d_bgd, d_w3, d_out = (sem(f"d_{n}") for n in ("bgu", "agd", "bgd", "w3", "out"))
        s_zero, s_iota, s_ident, s_chain, s_const = (sem(f"s_{n}") for n in ("zero", "iota", "ident", "chain", "const"))
        s_tb, s_eb, s_ta, s_ea, s_tw, s_wh, s_wl = (sem(f"s_{n}") for n in ("tb", "eb", "ta", "ea", "tw", "wh", "wl"))
        s_w2h, s_perm, s_two = sem("s_w2h"), sem("s_perm"), sem("s_two")
        s_xh, s_xl, s_w0i, s_w0h, s_w0l = (sem(f"s_{n}") for n in ("xh", "xl", "w0i", "w0h", "w0l"))
        s_ag1h, s_ag1l, s_aguh, s_agul, s_agdh, s_agdl = (sem(f"s_{n}") for n in ("ag1h", "ag1l", "aguh", "agul", "agdh", "agdl"))
        s_w3h, s_w3l, s_meta = sem("s_w3h"), sem("s_w3l"), sem("s_meta")
        RING = ["gate0", "up0", "gate1", "up1", "gate2", "up2", "bg1", "bgd"]
        s_rh = {u: sem(f"s_rh_{u}") for u in RING}
        s_rl = {u: sem(f"s_rl_{u}") for u in RING}
        s_l0, s_l1a, s_l1b, s_ag, s_au = (sem(f"s_{n}") for n in ("l0", "l1a", "l1b", "ag", "au"))
        s_gate = [sem(f"s_gate{j}") for j in range(3)]
        s_up = [sem(f"s_up{j}") for j in range(3)]
        s_tr = [sem(f"s_tr{j}") for j in range(3)]
        s_dn = [sem(f"s_dn{j}") for j in range(3)]
        s_ad, s_x3, s_o = sem("s_ad"), sem("s_x3"), sem("s_o")
        s_h = [sem(f"s_h{j}") for j in range(2)]
        s_x1h, s_x1l, s_x2h, s_x2l = (sem(f"s_{n}") for n in ("x1h", "x1l", "x2h", "x2l"))
        s_tm, s_sum, s_hh, s_tms, s_ts = ({c: sem(f"s_{n}_{c}") for c in ts} for n in ("tm", "sum", "hh", "tms", "ts"))
        s_sil = [sem(f"s_sil{j}") for j in range(3)]
        s_mul = [sem(f"s_mul{j}") for j in range(3)]
        s_ath = [sem(f"s_ath{j}") for j in range(3)]
        s_atl = [sem(f"s_atl{j}") for j in range(3)]
        s_x3r, s_x3h, s_x3l = sem("s_x3r"), sem("s_x3h"), sem("s_x3l")
        s_gelu = [sem(f"s_gelu{j}") for j in range(2)]
        s_gh = [sem(f"s_gh{j}") for j in range(2)]
        s_gl = [sem(f"s_gl{j}") for j in range(2)]
        s_f1, s_f2, s_f3 = sem("s_f1"), sem("s_f2"), sem("s_f3")

        def seen(eng, s, count):
            if not (isinstance(count, int) and count == 0):
                eng.wait_ge(s, count)

        ring_src = {"bg1": (bg1, 0, 512), "bgd": (bgd, 0, 512)}
        for j, (f0, n) in enumerate(BLOCKS):
            ring_src[f"gate{j}"] = (bgu, f0, n)
            ring_src[f"up{j}"] = (bgu, F + f0, n)

        def ring_free(eng, u, g):
            i = RING.index(u)
            if u == "gate0":
                eng.wait_ge(s_l1b, g + 1)
            elif u == "up0":
                seen(eng, s_x3, g)
            elif u == "bg1":
                seen(eng, s_gate[2], g + 1)
            elif u == "bgd":
                eng.wait_ge(s_up[2], g + 1)
            else:
                eng.wait_ge((s_gate, s_up)[i % 2][i // 2 - 1], g + 1)

        def ring_views(u):
            src, o, n = ring_src[u]
            i = RING.index(u) % 2
            return src[:, o:o + n], ringh[:, i, 0:n], ringl[:, i, 0:n]

        def ring_loaded(eng, u, g):
            if u == "bg1":
                eng.wait_ge(d_bg1, 64 * (g + 2))
            elif u == "bgd":
                eng.wait_ge(d_bgd, 64 * (g + 1))
            else:
                eng.wait_ge(d_bgu, 64 * (g + 1))

        def ring_count(u, g):
            return g + 2 if u == "bg1" else g + 1

        def loop(eng, step):
            step(0, False, True)
            with eng.Fori(1, G - 1) as g:
                step(g, True, True)
            step(G - 1, True, False)

        def weight_out(w, low):
            src = bank[w % 8]
            if w < 24:
                t, k, j = w // 12, (w % 12) // 3, w % 3
                f0, n = BLOCKS[j]
                return (wguh, wgul)[low][:, k, t * F + f0:t * F + f0 + n], src[:, 0:n]
            c = w - 24
            n = P if c < FC - 1 else FLAST
            return (wdh, wdl)[low][0:n, c, :], src[0:n, :]

        def parts(split):
            v = split[:].rearrange("p k (b c r) -> p c k b r", b=NBG, c=2)
            return v[:, 0], v[:, 1]

        SUM = {"t1": GATE[1], "td": M, "tg": GATE[1], "tu": UP[1]}

        def stack_before(eng, c, n, alone=False):
            if c == "t1":
                seen(eng, s_ts["tu"], n)
            elif c == "td":
                eng.wait_ge(s_ts["tu"], n + 1) if alone else eng.wait_ge(s_ts["t1"], n + 2)
            elif c == "tg":
                eng.wait_ge(s_ts["t1"], 1) if alone else eng.wait_ge(s_ts["td"], n)
            else:
                eng.wait_ge(s_ts["tg"], n + 1)

        x_rows = x.rearrange("b c t -> (b c) t")
        out_rows = out.rearrange("b c t -> (b c) t")
        block = ctx.enter_context(nc.Block())

        @block.sync
        def _(sp):
            for i, c in enumerate((c0, c1, c2, c3)):
                sp.dma_start(idx[i:i + 1, :], c.rearrange("(o b) -> o b", o=1)).then_inc(d_small, 16)
            for dst, src in ((nbg, Bg), (nbu, Bu)):
                v = src[0].rearrange("a (p q) r -> p a (q r)", q=FQ)
                sp.dma_start(dst[0:80], v[0:80]).then_inc(d_bn, 16)
                sp.dma_start(dst[80:FP], v[80:FP]).then_inc(d_bn, 16)
            sp.dma_start(nbd[:], Bd[0].rearrange("a (p q) r -> p a (q r)", q=KH)).then_inc(d_bn, 16)
            sp.dma_start(nb1[:], A1.rearrange("a (p q) r -> p a (q r)", q=KH)).then_inc(d_bn, 16)
            sp.dma_start(na1[:], B1.rearrange("a r h -> (a r) h")).then_inc(d_an, 16)
            for dst, src in ((nag, Ag), (nau, Au), (nad, Ad)):
                sp.dma_start(dst[:], src[0].rearrange("(s a) r h -> (a r) s h", s=2)).then_inc(d_an, 16)
            for dst, src in ((nwg, Wg), (nwu, Wu)):
                n = (FC - 1) * P
                sp.dma_start(dst[:, 0:FC - 1, :], src[0:n, :].rearrange("(c p) h -> p c h", p=P)).then_inc(d_wn, 16)
                sp.dma_start(dst[0:FLAST, FC - 1, :], src[n:F, :]).then_inc(d_wn, 16)

            sp.wait_ge(s_eb, 19)
            for part in range(2):
                for s in range(2):
                    sp.dma_start(scr_b2[8 * s:8 * s + 8, part].rearrange("a r n -> a r n"), rows2[:, s, :]).then_inc(d_scr, 16)
                sp.dma_start(scr_b1[:, part], rows1[:]).then_inc(d_scr, 16)
            sp.wait_ge(s_ea, 11)
            sp.dma_start(scr_a2.rearrange("a p n -> p a n"), tab2[:]).then_inc(d_scr, 16)
            sp.dma_start(scr_a1.rearrange("a p n -> p a n"), tab1[:]).then_inc(d_scr, 16)
            sp.wait_ge(s_tw, 12)
            sp.dma_start(nwd[:], Wd.rearrange("(c p) f -> p c f", p=P)).then_inc(d_wn, 16)
            sp.wait_ge(d_scr, 128)
            sp.wait_ge(d_small, 16 * 15)
            sp.wait_ge(s_zero, 3)
            sp.wait_ge(s_wl, 35)

            def chosen(row, n, k):
                return [sp.value_load(idx[row:row + 1, bass.ds(NBG * n + b, 1)], min_val=0, max_val=k - 1)
                        for b in range(NBG)]

            def load_x(n):
                seen(sp, s_xh, n)
                seen(sp, s_xl, n)
                sp.dma_start(xraw[:], x_rows[bass.ds(n * P, P), :]).then_inc(d_x, 16)

            def load_w0(n):
                v = chosen(0, n, 16)
                seen(sp, s_w0i, n)
                for b in range(NBG):
                    q = slice(CH * b, CH * b + CH)
                    sp.dma_start(w0raw[q, q], W0[bass.ds(v[b], 1)].rearrange("a c d -> (a c) d")).then_inc(d_w0, 16)

            def load_rank1(n):
                v = chosen(1, n, NA1)
                seen(sp, s_ag1l, n)
                for b in range(NBG):
                    sp.dma_start(ag1r[:, b, :], scr_a1[bass.ds(v[b], 1)].rearrange("a p n -> (a p) n")).then_inc(d_ag1, 16)
                seen(sp, s_rl["bg1"], n)
                for b in range(NBG):
                    sp.dma_start(bg1[CH * b:CH * b + CH, :],
                                 scr_b1[bass.ds(v[b], 1)].rearrange("a c r n -> (a c r) n")).then_inc(d_bg1, 16)

            def load_agu(n):
                v = chosen(2, n, NA2)
                seen(sp, s_agul, n)
                for b in range(NBG):
                    sp.dma_start(agur[:, b, :], scr_a2[bass.ds(v[b], 1), :, 0:AGU].rearrange("a p n -> (a p) n")).then_inc(d_agu, 16)

            def load_bgu(n):
                v = chosen(2, n, NA2)
                seen(sp, s_rl["up2"], n)
                for b in range(NBG):
                    sp.dma_start(bgu[CH * b:CH * b + CH, :],
                                 scr_b2[bass.ds(v[b], 1), :, :, 0:2 * F].rearrange("a c r n -> (a c r) n")).then_inc(d_bgu, 16)

            def load_down(g):
                v = chosen(2, g, NA2)
                seen(sp, s_agdl, g)
                for b in range(NBG):
                    sp.dma_start(agdr[:, b, :], scr_a2[bass.ds(v[b], 1), :, AGU:AGU + AGD].rearrange("a p n -> (a p) n")).then_inc(d_agd, 16)
                seen(sp, s_rl["bgd"], g)
                for b in range(NBG):
                    sp.dma_start(bgd[CH * b:CH * b + CH, :],
                                 scr_b2[bass.ds(v[b], 1), :, :, 2 * F:BROW].rearrange("a c r n -> (a c r) n")).then_inc(d_bgd, 16)

            def load_w3(g):
                v = chosen(3, g, NS)
                seen(sp, s_w3l, g)
                for b in range(NBG):
                    sp.dma_start(w3raw[CH * b:CH * b + CH, HID * b:HID * b + HID],
                                 W3[bass.ds(v[b], 1)].rearrange("a c d -> (a c) d")).then_inc(d_w3, 16)

            def store(g, count):
                sp.wait_ge(s_f3, count)
                sp.dma_start(out_rows[bass.ds(g * P, P), :], x3raw[:]).then_inc(d_out, 16)

            load_x(0)
            load_w0(0)
            load_rank1(0)
            load_agu(0)
            load_bgu(0)

            def step(g, prev, nxt):
                load_down(g)
                if nxt:
                    load_x(g + 1)
                    load_w0(g + 1)
                    load_rank1(g + 1)
                    load_agu(g + 1)
                load_w3(g)
                if prev:
                    store(g - 1, g)
                if nxt:
                    load_bgu(g + 1)

            loop(sp, step)
            store(G - 1, G)
            sp.wait_ge(d_out, 16 * G)

        @block.gpsimd
        def _(pool):
            nc.gpsimd.memset(w0raw[:], 0.0).then_inc(s_zero, 1)
            nc.gpsimd.memset(w3raw[:], 0.0).then_inc(s_zero, 1)
            nc.gpsimd.memset(w2raw[:], 0.0).then_inc(s_zero, 1)
            nc.gpsimd.iota(pidx[:, 0:1], pattern=[[0, 1]], base=0, channel_multiplier=1).then_inc(s_iota, 1)
            nc.gpsimd.iota(iota_t[:], pattern=[[1, T]], base=0, channel_multiplier=0).then_inc(s_iota, 1)
            nc.gpsimd.memset(ident[:], 0.0).then_inc(s_ident, 1)
            pool.wait_ge(s_ident, 1)
            nc.gpsimd.affine_select(out=ident[:], in_=ident[:], compare_op=ALU.not_equal, fill=1.0, base=0,
                                    pattern=[[-1, P]], channel_multiplier=1).then_inc(s_ident, 1)
            nc.gpsimd.memset(both[:], 0.0).then_inc(s_two, 1)
            for i, shift in enumerate((0, RK, -RK)):
                pool.wait_ge(s_two, i + 1)
                nc.gpsimd.affine_select(out=both[:], in_=both[:], compare_op=ALU.not_equal, fill=1.0, base=shift,
                                        pattern=[[-1, P]], channel_multiplier=1).then_inc(s_two, 1)
            pool.wait_ge(d_bn, 96)
            nc.gpsimd.tensor_copy(pbd[:].rearrange("p q a r -> p a q r"), nbd[:].rearrange("p a (q r) -> p a q r", r=RK)).then_inc(s_perm, 1)
            nc.gpsimd.tensor_copy(pb1[:].rearrange("p q a r -> p a q r"), nb1[:].rearrange("p a (q r) -> p a q r", r=RK)).then_inc(s_perm, 1)
            pool.wait_ge(s_zero, 3)
            pool.wait_ge(s_ident, 2)

            def low(dst, src, high, s):
                nc.gpsimd.tensor_tensor(dst, src, f(high), ALU.subtract).then_inc(s, 1)

            def ring_low(u, g):
                ring_loaded(pool, u, g)
                pool.wait_ge(s_rh[u], ring_count(u, g))
                src, h, l = ring_views(u)
                low(l, src, h, s_rl[u])

            def x_low(n):
                pool.wait_ge(s_xh, n + 1)
                low(xsl[:], xraw[:], xsh[:], s_xl)

            def w0_low(n):
                pool.wait_ge(d_w0, 64 * (n + 1))
                seen(pool, s_w0l, n)
                nc.gpsimd.tensor_tensor(w0i[:], w0raw[:], ident[:], ALU.add).then_inc(s_w0i, 1)
                pool.wait_ge(s_w0i, n + 1)
                pool.wait_ge(s_w0h, n + 1)
                low(w0l[:], w0i[:], w0h[:], s_w0l)

            def gathered_low(dst, raw, s_high, s_low, n):
                pool.wait_ge(s_high, n + 1)
                high, lo = parts(dst)
                nc.gpsimd.tensor_tensor(lo, raw[:].rearrange("p b (k r) -> p k b r", r=RK), f(high),
                                        ALU.subtract).then_inc(s_low, 1)

            x_low(0)
            w0_low(0)
            gathered_low(ag1, ag1r, s_ag1h, s_ag1l, 0)
            ring_low("bg1", -1)
            gathered_low(agu, agur, s_aguh, s_agul, 0)

            def step(g, prev, nxt):
                ring_low("gate0", g)
                ring_low("up0", g)
                ring_low("gate1", g)
                gathered_low(agd, agdr, s_agdh, s_agdl, g)
                ring_low("up1", g)
                if nxt:
                    x_low(g + 1)
                    w0_low(g + 1)
                    gathered_low(ag1, ag1r, s_ag1h, s_ag1l, g + 1)
                ring_low("gate2", g)
                ring_low("up2", g)
                if nxt:
                    ring_low("bg1", g)
                    gathered_low(agu, agur, s_aguh, s_agul, g + 1)
                ring_low("bgd", g)

            loop(pool, step)

        @block.scalar
        def _(act):
            act.wait_ge(s_zero, 3)
            for half in range(2):
                q = slice(HID * half, HID * half + HID)
                act.dma_start(w2raw[q, HID + CH * half:HID + CH * half + CH], W2).then_inc(d_small, 16)
                act.dma_start(b3t[q, :], b3.rearrange("a h -> h a")).then_inc(d_small, 16)
            for b in range(NBG):
                act.dma_start(b2col[CH * b:CH * b + CH, :], b2.rearrange("(s o) -> s o", o=1)).then_inc(d_small, 16)
            for dst, src in ((bci, c3), (bcc, chans), (bcs, seqlen)):
                act.dma_start(dst[:], src.partition_broadcast(P)).then_inc(d_small, 16)
            act.wait_ge(d_bn, 96)
            nc.scalar.copy(pbu[:].rearrange("p q a r -> p a q r"), nbu[:].rearrange("p a (q r) -> p a q r", r=RK)).then_inc(s_perm, 1)
            for u in range(11):
                act.wait_ge(s_ta, u + 1)
                src = bank[4 + u % 4]
                if u == 0:
                    last = nc.scalar.copy(tab1[:].rearrange("p a (k r) -> p k a r", r=RK),
                                          src[:].rearrange("p (k a r) -> p k a r", k=KH, r=RK))
                elif u < 5:
                    which, s = (u - 1) // 2, (u - 1) % 2
                    dst = tab2[:, 8 * s:8 * s + 8, which * KH * RK:(which + 1) * KH * RK]
                    last = nc.scalar.copy(dst.rearrange("p a (k r) -> p k a r", r=RK),
                                          src[:].rearrange("p (k a r) -> p k a r", k=KH, r=RK))
                else:
                    s, j = (u - 5) // 3, (u - 5) % 3
                    full = 4 if j < 2 else 2
                    c = 4 * j
                    dst = tab2[:, 8 * s:8 * s + 8, AGU + c * RK:AGU + (c + full) * RK]
                    last = nc.scalar.copy(dst.rearrange("p a (k r) -> p k a r", r=RK),
                                          src[:, 0:full * P].rearrange("p (k a r) -> p k a r", k=full, r=RK))
                    if j == 2:
                        c = FC - 1
                        last = nc.scalar.copy(tab2[0:FLAST, 8 * s:8 * s + 8, AGU + c * RK:AGU + (c + 1) * RK],
                                              src[0:FLAST, 2 * P:3 * P].rearrange("p (a r) -> p a r", r=RK))
                last.then_inc(s_ea, 1)
            act.wait_ge(d_scr, 128)
            for w in range(35):
                act.wait_ge(s_tw, w + 1)
                if w == 0:
                    act.wait_ge(s_const, 1)
                dst, src = weight_out(w, 0)
                nc.scalar.copy(dst, src).then_inc(s_wh, 1)
            act.wait_ge(d_small, 16 * 15)
            nc.scalar.copy(w2h[:], w2raw[:]).then_inc(s_w2h, 1)

            def copy(dst, src, s):
                nc.scalar.activation(dst, src, ACT.Copy).then_inc(s, 1)

            def ring_high(u, g):
                ring_loaded(act, u, g)
                ring_free(act, u, g)
                src, h, _ = ring_views(u)
                copy(h, src, s_rh[u])

            def x_high(n):
                act.wait_ge(d_x, 16 * (n + 1))
                if isinstance(n, int) and n <= 1:
                    seen(act, s_l0, n)
                else:
                    act.wait_ge(s_h[1], n - 1)
                copy(xsh[:], xraw[:], s_xh)

            def w0_high(n):
                act.wait_ge(s_w0i, n + 1)
                seen(act, s_l0, n)
                copy(w0h[:], w0i[:], s_w0h)

            def gathered_high(dst, raw, d, used, s, n):
                act.wait_ge(d, 64 * (n + 1))
                seen(act, used, n)
                copy(parts(dst)[0], raw[:].rearrange("p b (k r) -> p k b r", r=RK), s)

            def stack_high(c, k, alone=False):
                act.wait_ge(s_sum[c], k + 1)
                stack_before(act, c, k, alone)
                copy(hh[:], SUM[c][:, P:2 * P], s_hh[c])

            def prepare_high(n):
                act.wait_ge(s_l0, n + 1)
                seen(act, s_l1a, n)
                copy(x1h, X[:], s_x1h)

            x_high(0)
            w0_high(0)
            gathered_high(ag1, ag1r, d_ag1, s_l1a, s_ag1h, 0)
            ring_loaded(act, "bg1", -1)
            _src, _h, _ = ring_views("bg1")
            copy(_h, _src, s_rh["bg1"])
            gathered_high(agu, agur, d_agu, s_au, s_aguh, 0)
            prepare_high(0)
            stack_high("t1", 0)
            act.wait_ge(s_l1b, 1)
            copy(x2h[:], X[:], s_x2h)
            stack_high("tg", 0, True)
            stack_high("tu", 0)

            def silu(j, g):
                act.wait_ge(s_gate[j], g + 1)
                if j:
                    act.wait_ge(s_mul[j - 1], g + 1)
                else:
                    seen(act, s_mul[2], g)
                n = BLOCKS[j][1]
                nc.scalar.activation(sil[:, 0:n], GATE[j][:, 0:n], ACT.Silu).then_inc(s_sil[j], 1)

            def act_high(j, g):
                act.wait_ge(s_tr[j], g + 1)
                if j == 2:
                    act.wait_ge(s_dn[0], g + 1)
                else:
                    seen(act, s_dn[2 if j == 0 else 1], g)
                nf = -(-BLOCKS[j][1] // P) * P
                if j == 2:
                    nc.scalar.activation(ath[:, 0, 0:2 * P], TP[:, 0:2 * P], ACT.Copy)
                    copy(ath[0:FLAST, 0, 2 * P:3 * P], TP[0:FLAST, 2 * P:3 * P], s_ath[j])
                else:
                    copy(ath[:, j, 0:nf], TP[:, 0:nf], s_ath[j])

            def gelu(half, g):
                act.wait_ge(s_h[half], g + 1)
                seen(act, s_f3, g)
                nc.scalar.activation(graw[:, half, :], HB[half][:], ACT.Gelu,
                                     bias=cols[:, 2 + half:3 + half]).then_inc(s_gelu[half], 1)

            def gelu_high(half, g):
                act.wait_ge(s_gelu[half], g + 1)
                seen(act, s_o, g)
                copy(gh[:, half, :], graw[:, half, :], s_gh[half])

            def last_layer_a(g):
                gelu(0, g)
                gelu(1, g)
                gelu_high(0, g)
                gelu_high(1, g)

            def last_layer_b(g):
                act.wait_ge(s_o, g + 1)
                act.wait_ge(s_gl[0], g + 1)
                nc.scalar.activation(graw[:, 0, :], M[:], ACT.Identity, bias=b2col[:, 0:1]).then_inc(s_f1, 1)

            def w3_high(g):
                act.wait_ge(d_w3, 64 * (g + 1))
                act.wait_ge(s_meta, g + 1)
                seen(act, s_h[1], g)
                nc.scalar.activation(w3h[:], w3raw[:], ACT.Copy, scale=cols[:, 0:1]).then_inc(s_w3h, 1)

            def step(g, prev, nxt):
                ring_high("gate0", g)
                ring_high("up0", g)
                silu(0, g)
                ring_high("gate1", g)
                gathered_high(agd, agdr, d_agd, s_ad, s_agdh, g)
                if prev:
                    last_layer_a(g - 1)
                ring_high("up1", g)
                if nxt:
                    x_high(g + 1)
                    w0_high(g + 1)
                    gathered_high(ag1, ag1r, d_ag1, s_l1a, s_ag1h, g + 1)
                silu(1, g)
                ring_high("gate2", g)
                ring_high("up2", g)
                act_high(0, g)
                if prev:
                    last_layer_b(g - 1)
                silu(2, g)
                if nxt:
                    ring_high("bg1", g)
                    gathered_high(agu, agur, d_agu, s_au, s_aguh, g + 1)
                    prepare_high(g + 1)
                act_high(1, g)
                ring_high("bgd", g)
                w3_high(g)
                if nxt:
                    stack_high("t1", g + 1)
                act_high(2, g)
                if nxt:
                    act.wait_ge(s_l1b, g + 2)
                    copy(x2h[:], X[:], s_x2h)
                stack_high("td", g, not nxt)
                if nxt:
                    stack_high("tg", g + 1)
                    stack_high("tu", g + 1)
                act.wait_ge(s_x3r, g + 1)
                copy(xsh[:], x3raw[:], s_x3h)

            loop(act, step)
            last_layer_a(G - 1)
            last_layer_b(G - 1)

        @block.vector
        def _(dve):
            chain = [0]

            def link(ins):
                chain[0] += 1
                ins.then_inc(s_chain, 1)
                dve.wait_ge(s_chain, chain[0])

            link(nc.vector.memset(tab2[FLAST:P, :, AGU + AGD - RK:AGU + AGD], 0.0))
            link(nc.vector.memset(mask[:], 0.0))
            for b in range(NBG):
                q = slice(CH * b, CH * b + CH)
                link(nc.vector.memset(mask[q, q], 1.0))
            dve.wait_ge(s_iota, 2)
            dve.wait_ge(s_ident, 2)
            link(nc.vector.tensor_copy(ident_r[:], ident[:]))
            link(nc.vector.tensor_scalar(pidx[:, 1:2], pidx[:, 0:1], CH - 1, None, ALU.bitwise_and))
            link(nc.vector.tensor_scalar(pidx[:, 2:3], pidx[:, 0:1], 4, 1, ALU.logical_shift_right, ALU.bitwise_and))
            link(nc.vector.tensor_copy(colf[:, 0:2], pidx[:, 1:3]))
            link(nc.vector.tensor_scalar(colf[:, 2:3], colf[:, 1:2], -2.0, 1.0, ALU.mult, ALU.add))
            dve.wait_ge(s_two, 4)
            link(nc.vector.tensor_tensor(both[:], both[:], mask[:], ALU.mult))
            dve.wait_ge(d_bn, 96)
            nc.vector.tensor_copy(pbg[:].rearrange("p q a r -> p a q r"), nbg[:].rearrange("p a (q r) -> p a q r", r=RK)).then_inc(s_perm, 1)
            for u in range(19):
                dve.wait_ge(s_tb, u + 1)
                src = bank[u % 4]
                if u < 16:
                    t, s, q = u // 8, (u // 4) % 2, u % 4
                    dst = rows2[:, s, t * F:(t + 1) * F].rearrange("p (m q i) -> p q i m", q=4, i=4)[:, q]
                    last = nc.vector.tensor_copy(dst, src[:, 0:4 * FP].rearrange("p (i m) -> p i m", i=4))
                elif u < 18:
                    dst = rows2[:, u - 16, 2 * F:BROW].rearrange("p (m i) -> p i m", i=KH)
                    last = nc.vector.tensor_copy(dst, src[:].rearrange("p (i m) -> p i m", i=KH))
                else:
                    last = nc.vector.tensor_copy(rows1[:].rearrange("p (m i) -> p i m", i=KH),
                                                 src[:].rearrange("p (i m) -> p i m", i=KH))
                last.then_inc(s_eb, 1)
            dve.wait_ge(d_small, 16 * 15)
            for b in range(NBG):
                q = slice(CH * b, CH * b + CH)
                link(nc.vector.tensor_scalar(meta[q, :, 0], bcc[q, :].rearrange("p (g b) -> p b g", b=NBG)[:, b],
                                             colf[q, 0:1], None, ALU.is_gt))
                link(nc.vector.tensor_copy(meta[q, :, 1], bcs[q, :].rearrange("p (g b) -> p b g", b=NBG)[:, b]))
            for half in range(2):
                q = slice(HID * half, HID * half + HID)
                which = bci[q, :].rearrange("p (g s b) -> p b g s", s=2, b=2)[:, half]
                for a in range(NS):
                    dst = btmp[q] if a else meta[q, :, 2:4]
                    link(nc.vector.tensor_scalar(dst, which, float(a), b3t[q, a:a + 1], ALU.is_equal, ALU.mult))
                    if a:
                        link(nc.vector.tensor_tensor(meta[q, :, 2:4], meta[q, :, 2:4], btmp[q], ALU.add))
            nc.vector.tensor_copy(cols[:], meta[:, 0, :]).then_inc(s_const, 1)
            for w in range(35):
                dve.wait_ge(s_wh, w + 1)
                dst, src = weight_out(w, 1)
                high, _ = weight_out(w, 0)
                nc.vector.tensor_tensor(dst, src, f(high), ALU.subtract).then_inc(s_wl, 1)
            dve.wait_ge(s_w2h, 1)
            link(nc.vector.tensor_tensor(w2l[:], w2raw[:], f(w2h[:]), ALU.subtract))

            def low(dst, src, high, s):
                nc.vector.tensor_tensor(dst, src, f(high), ALU.subtract).then_inc(s, 1)

            def masked(c, psum, scale, k):
                nc.vector.scalar_tensor_tensor(out=tm[c][:], in0=psum, scalar=scale, in1=mask[:],
                                               op0=ALU.mult, op1=ALU.mult).then_inc(s_tm[c], 1)

            def stack(c, k, alone=False):
                dve.wait_ge(s_hh[c], k + 1)
                stack_before(dve, c, k, alone)
                nc.vector.tensor_scalar(tms[:], SUM[c][:, P:2 * P], colf[:, 1:2], None, ALU.mult).then_inc(s_tms[c], 1)
                dve.wait_ge(s_tms[c], k + 1)
                nc.vector.scalar_tensor_tensor(out=ts[c][:], in0=f(hh[:]), scalar=colf[:, 2:3], in1=tms[:],
                                               op0=ALU.mult, op1=ALU.add).then_inc(s_ts[c], 1)

            def masked_t1(n):
                dve.wait_ge(s_l1a, n + 1)
                seen(dve, s_sum["tg"], n)
                masked("t1", GATE[1][:, 0:P], 1.0, n)

            def stack_t1(n):
                seen(dve, s_l1b, n)
                stack("t1", n)

            def masked_td(g):
                dve.wait_ge(s_ad, g + 1)
                dve.wait_ge(s_sum["tu"], g + 1)
                masked("td", M[:, 0:P], 0.5, g)

            def stack_td(g, alone):
                seen(dve, s_x3, g)
                stack("td", g, alone)

            def masked_gu(n):
                dve.wait_ge(s_ag, n + 1)
                dve.wait_ge(s_sum["t1"], n + 1)
                masked("tg", GATE[1][:, 0:P], 0.5, n)
                dve.wait_ge(s_au, n + 1)
                seen(dve, s_sum["td"], n)
                masked("tu", UP[1][:, 0:P], 0.5, n)

            def stack_gu(n, alone=False):
                seen(dve, s_gate[2], n)
                stack("tg", n, alone)
                seen(dve, s_up[2], n)
                stack("tu", n)

            def x1_low(n):
                dve.wait_ge(s_x1h, n + 1)
                low(x1l, X[:], x1h, s_x1l)

            def x2_low(n):
                dve.wait_ge(s_x2h, n + 1)
                low(x2l[:], X[:], x2h[:], s_x2l)

            x1_low(0)
            masked_t1(0)
            stack_t1(0)
            x2_low(0)
            masked_gu(0)
            stack_gu(0, True)

            def mul(j, g):
                dve.wait_ge(s_sil[j], g + 1)
                dve.wait_ge(s_up[j], g + 1)
                if j:
                    dve.wait_ge(s_tr[j - 1], g + 1)
                else:
                    seen(dve, s_tr[2], g)
                n = BLOCKS[j][1]
                nc.vector.tensor_tensor(act_[:, 0:n], UP[j][:, 0:n], sil[:, 0:n], ALU.mult).then_inc(s_mul[j], 1)

            def act_low(j, g):
                dve.wait_ge(s_ath[j], g + 1)
                if j == 2:
                    nc.vector.tensor_tensor(atl[:, 0, 0:2 * P], TP[:, 0:2 * P], f(ath[:, 0, 0:2 * P]), ALU.subtract)
                    low(atl[0:FLAST, 0, 2 * P:3 * P], TP[0:FLAST, 2 * P:3 * P], ath[0:FLAST, 0, 2 * P:3 * P], s_atl[j])
                else:
                    low(atl[:, j, :], TP[:], ath[:, j, :], s_atl[j])

            def gelu_low(g):
                for half in range(2):
                    dve.wait_ge(s_gh[half], g + 1)
                    low(gl[:, half, :], graw[:, half, :], gh[:, half, :], s_gl[half])

            def finish(g):
                dve.wait_ge(s_f1, g + 1)
                nc.vector.scalar_tensor_tensor(out=graw[:, 1, :], in0=iota_t[:], scalar=cols[:, 1:2], in1=graw[:, 0, :],
                                               op0=ALU.is_lt, op1=ALU.mult).then_inc(s_f2, 1)
                dve.wait_ge(s_f2, g + 1)
                nc.vector.tensor_tensor(x3raw[:], x3raw[:], graw[:, 1, :], ALU.add).then_inc(s_f3, 1)

            def next_cols(g):
                if isinstance(g, int) and g == 0:
                    dve.wait_ge(s_const, 1)
                nc.vector.tensor_copy(cols[:], meta[:, bass.ds(g, 1), :].rearrange("p g c -> p (g c)")).then_inc(s_meta, 1)

            def step(g, prev, nxt):
                mul(0, g)
                if prev:
                    gelu_low(g - 1)
                mul(1, g)
                act_low(0, g)
                if prev:
                    finish(g - 1)
                next_cols(g)
                mul(2, g)
                if nxt:
                    x1_low(g + 1)
                act_low(1, g)
                if nxt:
                    masked_t1(g + 1)
                    stack_t1(g + 1)
                dve.wait_ge(s_w3h, g + 1)
                nc.vector.scalar_tensor_tensor(out=w3l[:], in0=w3raw[:], scalar=cols[:, 0:1], in1=f(w3h[:]),
                                               op0=ALU.mult, op1=ALU.subtract).then_inc(s_w3l, 1)
                act_low(2, g)
                if nxt:
                    x2_low(g + 1)
                masked_td(g)
                if nxt:
                    masked_gu(g + 1)
                stack_td(g, not nxt)
                if nxt:
                    stack_gu(g + 1)
                dve.wait_ge(s_x3, g + 1)
                seen(dve, d_out, 16 * g if isinstance(g, int) else g * 16)
                nc.vector.tensor_copy(x3raw[:], D[:]).then_inc(s_x3r, 1)
                dve.wait_ge(s_x3h, g + 1)
                low(xsl[:], x3raw[:], xsh[:], s_x3l)

            loop(dve, step)
            gelu_low(G - 1)
            finish(G - 1)

        @block.tensor
        def _(pe):
            pe.wait_ge(s_ident, 2)

            def tr(dst, src, n):
                return nc.tensor.transpose(dst, src, ident[0:n, 0:n])

            def b_unit(u):
                if u == 0:
                    pe.wait_ge(s_perm, 4)
                if u >= 4:
                    pe.wait_ge(s_eb, u - 3)
                dst = bank[u % 4]
                for i in range(4):
                    if u < 16:
                        t, s, q = u // 8, (u // 4) % 2, u % 4
                        src = (pbg, pbu)[t][:, 4 * q + i, 8 * s:8 * s + 8, :].rearrange("p a r -> p (a r)")
                        last = tr(dst[:, i * FP:(i + 1) * FP], src, FP)
                    else:
                        src = pbd[:, i, 8 * (u - 16):8 * (u - 16) + 8, :] if u < 18 else pb1[:, i]
                        last = tr(dst[:, i * P:(i + 1) * P], src.rearrange("p a r -> p (a r)"), P)
                last.then_inc(s_tb, 1)

            def a_unit(u):
                if u == 0:
                    pe.wait_ge(d_an, 64)
                if u >= 4:
                    pe.wait_ge(s_ea, u - 3)
                dst = bank[4 + u % 4]
                if u == 0:
                    pieces = [(na1[:, k * P:(k + 1) * P], P) for k in range(KH)]
                elif u < 5:
                    which, s = (u - 1) // 2, (u - 1) % 2
                    pieces = [((nag, nau)[which][:, s, k * P:(k + 1) * P], P) for k in range(KH)]
                else:
                    s, j = (u - 5) // 3, (u - 5) % 3
                    pieces = [(nad[:, s, c * P:min(F, (c + 1) * P)], min(P, F - c * P)) for c in range(4 * j, min(FC, 4 * j + 4))]
                for i, (src, m) in enumerate(pieces):
                    last = tr(dst[0:m, i * P:(i + 1) * P], src, P)
                last.then_inc(s_ta, 1)

            for u in range(19):
                b_unit(u)
                if u < 11:
                    a_unit(u)
            pe.wait_ge(s_ea, 11)
            pe.wait_ge(s_eb, 19)
            pe.wait_ge(d_wn, 64)
            for w in range(35):
                if w == 24:
                    pe.wait_ge(d_wn, 80)
                if w >= 8:
                    pe.wait_ge(s_wl, w - 7)
                dst = bank[w % 8]
                if w < 24:
                    t, k, j = w // 12, (w % 12) // 3, w % 3
                    for c in range(4 * j, min(FC, 4 * j + 4)):
                        m = min(P, F - c * P)
                        o = (c - 4 * j) * P
                        last = tr(dst[:, o:o + m], (nwg, nwu)[t][0:m, c, k * P:(k + 1) * P], m)
                else:
                    c = w - 24
                    m = min(P, F - c * P)
                    for k in range(KH):
                        last = tr(dst[0:m, k * P:(k + 1) * P], nwd[:, k, c * P:c * P + m], P)
                last.then_inc(s_tw, 1)

            def passes(dst, sh, sl, mh, ml, first, last_):
                nc.tensor.matmul(dst, sh, mh, start=first, stop=False)
                nc.tensor.matmul(dst, sl, mh, start=False, stop=False)
                return nc.tensor.matmul(dst, sh, ml, start=False, stop=last_)

            def rank_a(dst, split, k, h, l, first, last_):
                n = h.shape[0]
                nc.tensor.matmul(dst, split[0:n, k, :], h, start=first, stop=False)
                return nc.tensor.matmul(dst, split[0:n, k, :], l, start=False, stop=last_)

            def add_parts(c, k):
                pe.wait_ge(s_tm[c], k + 1)
                nc.tensor.matmul(SUM[c][:, P:2 * P], both[:], tm[c][:], start=True, stop=True).then_inc(s_sum[c], 1)

            def chunk(ap, k):
                return ap[:, k * P:(k + 1) * P]

            def layer0(n):
                pe.wait_ge(s_xl, n + 1)
                pe.wait_ge(s_w0l, n + 1)
                seen(pe, s_x2l, n)
                for k in range(KH):
                    last = passes(chunk(X, k), chunk(xsh, k), chunk(xsl, k), w0h[:], w0l[:], k == 0, k == KH - 1)
                last.then_inc(s_l0, 1)

            def layer1_a(n):
                pe.wait_ge(s_x1l, n + 1)
                pe.wait_ge(s_ag1l, n + 1)
                seen(pe, s_mul[1], n)
                for k in range(KH):
                    last = rank_a(GATE[1][:, 0:P], ag1, k, chunk(x1h, k), chunk(x1l, k), k == 0, k == KH - 1)
                last.then_inc(s_l1a, 1)

            def rank_b(dst, stat, u, n, first, last_):
                i = RING.index(u) % 2
                nc.tensor.matmul(dst, stat, ringh[:, i, 0:n], start=first, stop=False)
                return nc.tensor.matmul(dst, stat, ringl[:, i, 0:n], start=False, stop=last_)

            def layer1_b(n, g):
                pe.wait_ge(s_ts["t1"], n + 1)
                pe.wait_ge(s_rl["bg1"], n + 1)
                i = RING.index("bg1") % 2
                for k in range(KH):
                    for part in (ringh, ringl):
                        last = nc.tensor.matmul(chunk(X, k), part[:, i, k * P:(k + 1) * P], ts["t1"][:],
                                                start=False, stop=True, skip_group_check=True)
                last.then_inc(s_l1b, 1)

            def rank_gu_a(n):
                pe.wait_ge(s_x2l, n + 1)
                pe.wait_ge(s_agul, n + 1)
                for which, dst, s in ((0, GATE[1], s_ag), (1, UP[1], s_au)):
                    for k in range(KH):
                        last = rank_a(dst[:, 0:P], agu, which * KH + k, chunk(x2h, k), chunk(x2l, k), k == 0, k == KH - 1)
                    last.then_inc(s, 1)

            def gate_up(j, g):
                f0, n = BLOCKS[j]
                if j == 0:
                    seen(pe, s_mul[2], g)
                elif j == 2:
                    pe.wait_ge(s_mul[0], g + 1)
                else:
                    pe.wait_ge(s_ts["tu"], g + 1)
                for which, dst, c, s in ((0, GATE[j], "tg", s_gate), (1, UP[j], "tu", s_up)):
                    o = which * F + f0
                    for k in range(KH):
                        passes(dst[:, 0:n], chunk(x2h, k), chunk(x2l, k), wguh[:, k, o:o + n], wgul[:, k, o:o + n],
                               k == 0, False)
                    pe.wait_ge(s_ts[c], g + 1)
                    u = ("gate", "up")[which] + str(j)
                    pe.wait_ge(s_rl[u], g + 1)
                    rank_b(dst[:, 0:n], ts[c][:], u, n, False, True).then_inc(s[j], 1)

            def transpose_act(j, g):
                pe.wait_ge(s_mul[j], g + 1)
                if j:
                    pe.wait_ge(s_atl[j - 1], g + 1)
                else:
                    seen(pe, s_gelu[1], g)
                for i in range(-(-BLOCKS[j][1] // P)):
                    m = min(P, BLOCKS[j][1] - i * P)
                    last = tr(TP[0:m, i * P:(i + 1) * P], act_[:, i * P:i * P + m], P)
                last.then_inc(s_tr[j], 1)

            def residual(g):
                seen(pe, s_gelu[0], g)
                for k in range(KH):
                    nc.tensor.matmul(chunk(D, k), chunk(x2h, k), ident_r[:], start=(k == 0), stop=False)
                    nc.tensor.matmul(chunk(D, k), chunk(x2l, k), ident_r[:], start=False, stop=False)

            def down(j, g):
                pe.wait_ge(s_atl[j], g + 1)
                if j == 0:
                    pe.wait_ge(s_agdl, g + 1)
                    seen(pe, s_f1, g)
                slot = j % 2
                pieces = []
                for i in range(-(-BLOCKS[j][1] // P)):
                    c = 4 * j + i
                    m = min(P, F - c * P)
                    pieces.append((c, m) + tuple(a[0:m, slot, i * P:(i + 1) * P] for a in (ath, atl)))
                for c, m, h, l in pieces:
                    last = rank_a(M[:, 0:P], agd, c, h, l, c == 0, c == FC - 1)
                if j == 2:
                    last.then_inc(s_ad, 1)
                for c, m, h, l in pieces:
                    last = passes(D[:], h, l, wdh[0:m, c, :], wdl[0:m, c, :], False, False)
                last.then_inc(s_dn[j], 1)

            def rank_down_b(g):
                pe.wait_ge(s_ts["td"], g + 1)
                pe.wait_ge(s_rl["bgd"], g + 1)
                rank_b(D[:], ts["td"][:], "bgd", 512, False, True).then_inc(s_x3, 1)

            def layer3_a(g):
                pe.wait_ge(s_x3l, g + 1)
                pe.wait_ge(s_w3l, g + 1)
                for half in range(2):
                    passes(HB[half][:], chunk(w3h, half), chunk(w3l, half), xsh[:], xsl[:], True, True) \
                        .then_inc(s_h[half], 1)

            def layer3_b(g):
                for half in range(2):
                    pe.wait_ge(s_gl[half], g + 1)
                    o = HID * (1 - half)
                    last = passes(M[:], w2h[:, o:o + P], w2l[:, o:o + P], gh[:, half, :], gl[:, half, :], half == 0, half == 1)
                last.then_inc(s_o, 1)

            pe.wait_ge(s_wl, 35)
            layer0(0)
            layer1_a(0)
            add_parts("t1", 0)
            layer1_b(0, -1)
            rank_gu_a(0)
            add_parts("tg", 0)
            add_parts("tu", 0)

            def step(g, prev, nxt):
                gate_up(0, g)
                if prev:
                    layer3_a(g - 1)
                gate_up(1, g)
                transpose_act(0, g)
                if prev:
                    layer3_b(g - 1)
                gate_up(2, g)
                if nxt:
                    layer0(g + 1)
                transpose_act(1, g)
                residual(g)
                down(0, g)
                if nxt:
                    layer1_a(g + 1)
                transpose_act(2, g)
                if nxt:
                    add_parts("t1", g + 1)
                down(1, g)
                if nxt:
                    layer1_b(g + 1, g)
                down(2, g)
                if nxt:
                    rank_gu_a(g + 1)
                add_parts("td", g)
                if nxt:
                    add_parts("tg", g + 1)
                    add_parts("tu", g + 1)
                rank_down_b(g)

            loop(pe, step)
            layer3_a(G - 1)
            layer3_b(G - 1)


_INS = ["x", "itok_B_0_15", "itok_B_3_7", "itok_B_2_6", "itok_B_0_7", "itok_B_2182_4065", "_lenS",
        "L0_cond_weights", "L1_cond_A", "L1_cond_B", "L2_cond_W_gate", "L2_cond_W_up", "L2_cond_W_down",
        "L2_cond_A_gate", "L2_cond_B_gate", "L2_cond_A_up", "L2_cond_B_up", "L2_cond_A_down",
        "L2_cond_B_down", "L3_cond_W_sess", "L3_cond_b_sess", "L3_cond_W2", "L3_cond_b2"]


def kernel(**inputs):
    import numpy as _np
    import concourse.bass as _bass
    import concourse.bacc as _bacc
    from concourse import mybir as _mybir
    from concourse.bass_utils import run_bass_kernel_spmd as _run

    nc = _bacc.Bacc("TRN2", target_bir_lowering=False, num_devices=1, dynamic_dma_scratch_size=1024)
    arrays, args = {}, []
    for name in _INS:
        a = _np.ascontiguousarray(inputs[name])
        arrays[f"in_{name}_dram"] = a
        args.append(nc.dram_tensor(f"in_{name}_dram", a.shape, _mybir.dt.from_np(a.dtype), kind="ExternalInput").ap())
    out = nc.dram_tensor("out_0_dram", (BATCH, CH, T), _mybir.dt.float32, kind="ExternalOutput").ap()
    build(nc, _bass, _mybir, *args, out)
    r = _run(nc, [arrays], core_ids=[0])
    return r.results[0]["out_0_dram"]
```

```python
BATCH, CH, T = 128, 32, 512
P = 128
NBG = P // CH
G = BATCH // NBG
KH = T // P
F = 1376
FC = -(-F // P)
FLAST = F - (FC - 1) * P
RK = 16
NA1, NA2, NS = 8, 16, 8
HID = 64
BLOCKS = [(0, 512), (512, 512), (1024, F - 1024)]
BROW = 2 * F + T
AGU, AGD = 2 * KH * RK, FC * RK
FQ = 16
FP = F // FQ


def build(nc, bass, mybir, x, c0, c1, c2, c3, seqlen, chans, W0, A1, B1, Wg, Wu, Wd, Ag, Bg, Au, Bu,
          Ad, Bd, W3, b3, W2, b2, out):
    from contextlib import ExitStack

    F32, R32, I32, I16 = mybir.dt.float32, mybir.dt.float32r, mybir.dt.int32, mybir.dt.int16
    ALU, ACT = mybir.AluOpType, mybir.ActivationFunctionType
    ctx = ExitStack()
    with ctx:
        ctx.enter_context(nc.allow_non_contiguous_dma(reason="small tables, once"))

        def sb(name, shape, dt):
            return ctx.enter_context(nc.sbuf_tensor(name, shape, dt))

        def sem(name):
            return ctx.enter_context(nc.semaphore(name))

        def f(ap):
            return ap.bitcast(F32)

        ident = sb("ident", [P, P], F32)
        mask = sb("mask", [P, P], F32)
        pidx = sb("pidx", [P, 4], I32)
        colf = sb("colf", [P, 4], F32)
        iota_t = sb("iota_t", [P, T], I16)
        meta = sb("meta", [P, G, 4], F32)
        cols = sb("cols", [P, 4], F32)
        scrap = sb("scrap", [P, 1], F32)
        b2col = sb("b2col", [P, 1], F32)
        idx = sb("idx", [4, BATCH], I32)
        w0raw = sb("w0raw", [P, P], F32)
        w0i = sb("w0i", [P, P], F32)
        w0h, w0l = sb("w0h", [P, P], R32), sb("w0l", [P, P], R32)
        w3raw = sb("w3raw", [P, NBG * HID], F32)
        w3h, w3l = sb("w3h", [P, NBG * HID], R32), sb("w3l", [P, NBG * HID], R32)
        w2h, w2l = sb("w2h", [P, 192], R32), sb("w2l", [P, 192], R32)

        at_w = nc.sbuf_base
        wguh, wgul = (sb(n, [P, KH, 2 * F], R32) for n in ("wguh", "wgul"))
        wdh, wdl = sb("wdh", [P, FC, T + P], R32), sb("wdl", [P, FC, T], R32)

        at_work = nc.sbuf_base
        xraw = sb("xraw", [P, T], F32)
        xsh, xsl = sb("xsh", [P, T], R32), sb("xsl", [P, T], R32)
        x2h, x2l = sb("x2h", [P, T], R32), sb("x2l", [P, T], R32)
        x3raw = sb("x3raw", [P, T], F32)
        ag1r, ag1 = sb("ag1r", [P, NBG, KH * RK], F32), sb("ag1", [P, KH, P], R32)
        agur, agu = sb("agur", [P, NBG, AGU], F32), sb("agu", [P, 2 * KH, P], R32)
        agdr, agd = sb("agdr", [P, NBG, AGD], F32), wdh[:, :, T:T + P]
        bg1 = sb("bg1", [P, T], F32)
        bg2 = sb("bg2", [P, BROW], F32)
        ringh, ringl = (sb(n, [P, 2, 512], R32) for n in ("ringh", "ringl"))
        tm = sb("tm", [P, 2 * P], F32)
        tsum_x, tsum_gu = sb("tsum_x", [P, P], F32), sb("tsum_gu", [P, 2 * P], F32)
        tsum = {"t1": tsum_x, "td": tsum_x, "gu": tsum_gu}
        hh, tms = sb("hh", [P, 2 * P], R32), sb("tms", [P, 2 * P], F32)
        ts_x, ts_gu = sb("ts_x", [P, P], R32), sb("ts_gu", [P, 2 * P], R32)
        ts = {"t1": ts_x, "td": ts_x, "gu": ts_gu}
        sil = sb("sil", [P, 512], F32)
        ath, atl = (sb(n, [P, 2, 512], R32) for n in ("ath", "atl"))
        x2row = sb("x2row", [P, T], F32)
        graw = sb("graw", [P, 2, T], F32)
        gh, gl = (sb(n, [P, 2, T], R32) for n in ("gh", "gl"))
        x1h, x1l = gh[:, 1, :], gl[:, 1, :]
        x1row = graw[:, 1, :]

        def at(place):
            here = [place]

            def alloc(name, shape, dt):
                n = 4
                for s in shape[1:]:
                    n *= s
                t = nc.alloc_sbuf_tensor_at(name, shape, dt, offset=here[0])
                here[0] += -(-n // 32) * 32
                return t
            return alloc

        st = at(at_w)
        nbg, nbu = (st(n, [FP, NA2, FQ * RK], F32) for n in ("nbg", "nbu"))
        nbd = st("nbd", [P, NA2, KH * RK], F32)
        nb1 = st("nb1", [P, NA1, KH * RK], F32)
        rows2 = st("rows2", [P, 2, BROW], F32)
        rows1 = st("rows1", [P, T], F32)
        nag, nau = (st(n, [P, 2, T], F32) for n in ("nag", "nau"))
        nad = st("nad", [P, 2, F], F32)
        na1 = st("na1", [P, T], F32)
        tab2 = st("tab2", [P, NA2, AGU + AGD], F32)
        tab1 = st("tab1", [P, NA1, KH * RK], F32)
        pbg = st("pbg", [FP, FQ, NA2, RK], F32)
        bci, bcc, bcs = (st(n, [P, BATCH], I32) for n in ("bci", "bcc", "bcs"))
        b3t = st("b3t", [P, NS], F32)
        btmp = st("btmp", [P, G, 2], F32)
        w2raw = st("w2raw", [P, 192], F32)
        st = at(at_work)
        nwg, nwu = (st(n, [P, FC, T], F32) for n in ("nwg", "nwu"))
        pbu = st("pbu", [FP, FQ, NA2, RK], F32)
        pbd = st("pbd", [P, KH, NA2, RK], F32)
        pb1 = st("pb1", [P, KH, NA1, RK], F32)
        nwd = at(at_work)("nwd", [P, KH, F], F32)

        scr_a1 = nc.dram_tensor("scr_a1", [NA1, P, KH * RK], F32, kind="Internal").ap()
        scr_a2 = nc.dram_tensor("scr_a2", [NA2, P, AGU + AGD], F32, kind="Internal").ap()
        scr_b1 = nc.dram_tensor("scr_b1", [NA1, RK, T], F32, kind="Internal").ap()
        scr_b2 = nc.dram_tensor("scr_b2", [NA2, RK, BROW], F32, kind="Internal").ap()

        bank = [ctx.enter_context(nc.psum_tensor(f"bank{i}", [P, 512], F32)) for i in range(8)]
        GATE = [bank[0], bank[2], bank[0]]
        UP = [bank[1], bank[3], bank[1]]
        X, TP, D, M = bank[4], bank[5], bank[6], bank[7]
        HB = [D, TP]
        R, C = bank[2], bank[3]
        HALF = T // 2
        COEF = {"t1": C[:, 0:P], "td": M[:, HALF:HALF + P], "gu": C[:, 0:2 * P]}
        TURNED = {"t1": C[:, P:2 * P], "td": TP[:, 0:P], "gu": C[:, 2 * P:4 * P]}

        d_small, d_bn, d_an, d_wn = sem("d_small"), sem("d_bn"), sem("d_an"), sem("d_wn")
        d_scr = sem("d_scr")
        d_x, d_w0, d_ag1, d_bg1, d_agu = (sem(f"d_{n}") for n in ("x", "w0", "ag1", "bg1", "agu"))
        d_bg2, d_agd, d_w3, d_out = (sem(f"d_{n}") for n in ("bg2", "agd", "w3", "out"))
        s_zero, s_iota, s_ident, s_chain, s_const = (sem(f"s_{n}") for n in ("zero", "iota", "ident", "chain", "const"))
        s_tb, s_eb, s_ta, s_ea, s_tw, s_wh, s_wl = (sem(f"s_{n}") for n in ("tb", "eb", "ta", "ea", "tw", "wh", "wl"))
        s_w2h, s_perm = sem("s_w2h"), sem("s_perm")
        s_xh, s_xl, s_w0i, s_w0h, s_w0l = (sem(f"s_{n}") for n in ("xh", "xl", "w0i", "w0h", "w0l"))
        s_ag1h, s_ag1l, s_aguh, s_agul, s_agdh, s_agdl = (sem(f"s_{n}") for n in ("ag1h", "ag1l", "aguh", "agul", "agdh", "agdl"))
        s_w3h, s_w3l, s_meta = sem("s_w3h"), sem("s_w3l"), sem("s_meta")
        RING = ["bgd", "gate0", "up0", "gate1", "up1", "gate2", "up2", "bg1"]
        s_rh = {u: sem(f"s_rh_{u}") for u in RING}
        s_rl = {u: sem(f"s_rl_{u}") for u in RING}
        s_l0, s_l1a, s_l1b, s_ga = (sem(f"s_{n}") for n in ("l0", "l1a", "l1b", "ga"))
        s_x1r, s_tx1, s_x2r, s_tx2, s_pre = (sem(f"s_{n}") for n in ("x1r", "tx1", "x2r", "tx2", "pre"))
        s_gate = [sem(f"s_gate{j}") for j in range(3)]
        s_up = [sem(f"s_up{j}") for j in range(3)]
        s_tr = [sem(f"s_tr{j}") for j in range(3)]
        s_dn = [sem(f"s_dn{j}") for j in range(3)]
        s_x3, s_o = sem("s_x3"), sem("s_o")
        s_h = [sem(f"s_h{j}") for j in range(2)]
        s_x1h, s_x1l, s_x2h, s_x2l = (sem(f"s_{n}") for n in ("x1h", "x1l", "x2h", "x2l"))
        s_tm, s_sum, s_tt, s_hh, s_tms, s_ts = ({c: sem(f"s_{n}_{c}") for c in ts}
                                                for n in ("tm", "sum", "tt", "hh", "tms", "ts"))
        s_sil = [sem(f"s_sil{j}") for j in range(3)]
        s_mul = [sem(f"s_mul{j}") for j in range(3)]
        s_ath = [sem(f"s_ath{j}") for j in range(3)]
        s_atl = [sem(f"s_atl{j}") for j in range(3)]
        s_x3r, s_x3h, s_x3l = sem("s_x3r"), sem("s_x3h"), sem("s_x3l")
        s_gelu = [sem(f"s_gelu{j}") for j in range(2)]
        s_gh = [sem(f"s_gh{j}") for j in range(2)]
        s_gl = [sem(f"s_gl{j}") for j in range(2)]
        s_f1, s_f2, s_f3 = sem("s_f1"), sem("s_f2"), sem("s_f3")

        def seen(eng, s, count):
            if not (isinstance(count, int) and count == 0):
                eng.wait_ge(s, count)

        ring_src = {"bg1": (bg1, 0, 512), "bgd": (bg2, 2 * F, 512)}
        for j, (f0, n) in enumerate(BLOCKS):
            ring_src[f"gate{j}"] = (bg2, f0, n)
            ring_src[f"up{j}"] = (bg2, F + f0, n)

        def ring_free(eng, u, g):
            i = RING.index(u)
            if u == "bgd":
                eng.wait_ge(s_up[2], g + 1)
            elif u == "gate0":
                eng.wait_ge(s_l1b, g + 1)
            elif u == "up0":
                seen(eng, s_x3, g)
            elif u == "bg1":
                seen(eng, s_gate[2], g + 1)
            else:
                j = int(u[-1])
                eng.wait_ge((s_gate if u.startswith("gate") else s_up)[j - 1], g + 1)

        def ring_views(u):
            src, o, n = ring_src[u]
            i = RING.index(u) % 2
            return src[:, o:o + n], ringh[:, i, 0:n], ringl[:, i, 0:n]

        def ring_loaded(eng, u, g):
            if u == "bg1":
                eng.wait_ge(d_bg1, 64 * (g + 2))
            else:
                eng.wait_ge(d_bg2, 64 * (g + 1))

        def ring_count(u, g):
            return g + 2 if u == "bg1" else g + 1

        def loop(eng, step):
            step(0, False, True)
            with eng.Fori(0, (G - 2) // 2) as pair:
                step(pair * 2 + 1, True, True)
                step(pair * 2 + 2, True, True)
            step(G - 1, True, False)

        def weight_out(w, low):
            src = bank[w % 8]
            if w < 24:
                t, k, j = w // 12, (w % 12) // 3, w % 3
                f0, n = BLOCKS[j]
                return (wguh, wgul)[low][:, k, t * F + f0:t * F + f0 + n], src[:, 0:n]
            c = w - 24
            n = P if c < FC - 1 else FLAST
            return (wdh, wdl)[low][0:n, c, 0:T], src[0:n, :]

        def parts(split):
            v = split[:].rearrange("p k (b c r) -> p c k b r", b=NBG, c=2)
            return v[:, 0], v[:, 1]

        def stack_before(eng, c, n, alone=False):
            if c == "t1":
                seen(eng, s_ts["gu"], n)
            elif c == "td":
                eng.wait_ge(s_ts["gu"], n + 1) if alone else eng.wait_ge(s_ts["t1"], n + 2)
            else:
                eng.wait_ge(s_ts["t1"], 1) if alone else eng.wait_ge(s_ts["td"], n)

        x_rows = x.rearrange("b c t -> (b c) t")
        out_rows = out.rearrange("b c t -> (b c) t")
        block = ctx.enter_context(nc.Block())

        @block.sync
        def _(sp):
            for i, c in enumerate((c0, c1, c2, c3)):
                sp.dma_start(idx[i:i + 1, :], c.rearrange("(o b) -> o b", o=1)).then_inc(d_small, 16)
            for dst, src in ((nbg, Bg), (nbu, Bu)):
                v = src[0].rearrange("a (p q) r -> p a (q r)", q=FQ)
                sp.dma_start(dst[0:80], v[0:80]).then_inc(d_bn, 16)
                sp.dma_start(dst[80:FP], v[80:FP]).then_inc(d_bn, 16)
            sp.dma_start(nbd[:], Bd[0].rearrange("a (p q) r -> p a (q r)", q=KH)).then_inc(d_bn, 16)
            sp.dma_start(nb1[:], A1.rearrange("a (p q) r -> p a (q r)", q=KH)).then_inc(d_bn, 16)
            sp.dma_start(na1[:], B1.rearrange("a r h -> (a r) h")).then_inc(d_an, 16)
            for dst, src in ((nag, Ag), (nau, Au), (nad, Ad)):
                sp.dma_start(dst[:], src[0].rearrange("(s a) r h -> (a r) s h", s=2)).then_inc(d_an, 16)
            for dst, src in ((nwg, Wg), (nwu, Wu)):
                n = (FC - 1) * P
                sp.dma_start(dst[:, 0:FC - 1, :], src[0:n, :].rearrange("(c p) h -> p c h", p=P)).then_inc(d_wn, 16)
                sp.dma_start(dst[0:FLAST, FC - 1, :], src[n:F, :]).then_inc(d_wn, 16)

            sp.wait_ge(s_eb, 19)
            for s in range(2):
                sp.dma_start(scr_b2[8 * s:8 * s + 8], rows2[:, s, :]).then_inc(d_scr, 16)
            sp.dma_start(scr_b1[:], rows1[:]).then_inc(d_scr, 16)
            sp.wait_ge(s_ea, 11)
            sp.dma_start(scr_a2.rearrange("a p n -> p a n"), tab2[:]).then_inc(d_scr, 16)
            sp.dma_start(scr_a1.rearrange("a p n -> p a n"), tab1[:]).then_inc(d_scr, 16)
            sp.wait_ge(s_tw, 12)
            sp.dma_start(nwd[:], Wd.rearrange("(c p) f -> p c f", p=P)).then_inc(d_wn, 16)
            sp.wait_ge(d_scr, 80)
            sp.wait_ge(d_small, 16 * 15)
            sp.wait_ge(s_zero, 3)
            sp.wait_ge(s_wl, 35)

            def chosen(row, n, k):
                return [sp.value_load(idx[row:row + 1, bass.ds(NBG * n + b, 1)], min_val=0, max_val=k - 1)
                        for b in range(NBG)]

            def twice(rows):
                return rows.broadcast_to([2, RK, rows.shape[2]])

            def load_x(n):
                seen(sp, s_xh, n)
                seen(sp, s_xl, n)
                sp.dma_start(xraw[:], x_rows[bass.ds(n * P, P), :]).then_inc(d_x, 16)

            def load_w0(n):
                v = chosen(0, n, 16)
                seen(sp, s_w0i, n)
                for b in range(NBG):
                    q = slice(CH * b, CH * b + CH)
                    sp.dma_start(w0raw[q, q], W0[bass.ds(v[b], 1)].rearrange("a c d -> (a c) d")).then_inc(d_w0, 16)

            def load_rank1(n):
                v = chosen(1, n, NA1)
                seen(sp, s_ag1l, n)
                for b in range(NBG):
                    sp.dma_start(ag1r[:, b, :], scr_a1[bass.ds(v[b], 1)].rearrange("a p n -> (a p) n")).then_inc(d_ag1, 16)
                seen(sp, s_rl["bg1"], n)
                for b in range(NBG):
                    sp.dma_start(bg1[CH * b:CH * b + CH, :], twice(scr_b1[bass.ds(v[b], 1)])).then_inc(d_bg1, 16)

            def load_rank2_a(n):
                v = chosen(2, n, NA2)
                seen(sp, s_agul, n)
                for b in range(NBG):
                    sp.dma_start(agur[:, b, :], scr_a2[bass.ds(v[b], 1), :, 0:AGU].rearrange("a p n -> (a p) n")).then_inc(d_agu, 16)
                seen(sp, s_agdl, n)
                for b in range(NBG):
                    sp.dma_start(agdr[:, b, :], scr_a2[bass.ds(v[b], 1), :, AGU:AGU + AGD].rearrange("a p n -> (a p) n")).then_inc(d_agd, 16)
                return v

            def load_rank2_b(v, n):
                seen(sp, s_rl["bgd"], n)
                for b in range(NBG):
                    sp.dma_start(bg2[CH * b:CH * b + CH, :], twice(scr_b2[bass.ds(v[b], 1)])).then_inc(d_bg2, 16)

            def load_w3(g):
                v = chosen(3, g, NS)
                seen(sp, s_w3l, g)
                for b in range(NBG):
                    sp.dma_start(w3raw[CH * b:CH * b + CH, HID * b:HID * b + HID],
                                 W3[bass.ds(v[b], 1)].rearrange("a c d -> (a c) d")).then_inc(d_w3, 16)

            def store(g, count):
                sp.wait_ge(s_f3, count)
                sp.dma_start(out_rows[bass.ds(g * P, P), :], x3raw[:]).then_inc(d_out, 16)

            load_x(0)
            load_w0(0)
            load_rank1(0)
            load_rank2_b(load_rank2_a(0), 0)

            def step(g, prev, nxt):
                if nxt:
                    load_x(g + 1)
                    load_w0(g + 1)
                    load_rank1(g + 1)
                load_w3(g)
                if nxt:
                    v = load_rank2_a(g + 1)
                if prev:
                    store(g - 1, g)
                if nxt:
                    load_rank2_b(v, g + 1)

            loop(sp, step)
            store(G - 1, G)
            sp.wait_ge(d_out, 16 * G)

        @block.gpsimd
        def _(pool):
            nc.gpsimd.memset(w0raw[:], 0.0).then_inc(s_zero, 1)
            nc.gpsimd.memset(w3raw[:], 0.0).then_inc(s_zero, 1)
            nc.gpsimd.memset(w2raw[:], 0.0).then_inc(s_zero, 1)
            nc.gpsimd.iota(pidx[:, 0:1], pattern=[[0, 1]], base=0, channel_multiplier=1).then_inc(s_iota, 1)
            nc.gpsimd.iota(iota_t[:], pattern=[[1, T]], base=0, channel_multiplier=0).then_inc(s_iota, 1)
            nc.gpsimd.memset(ident[:], 0.0).then_inc(s_ident, 1)
            pool.wait_ge(s_ident, 1)
            nc.gpsimd.affine_select(out=ident[:], in_=ident[:], compare_op=ALU.not_equal, fill=1.0, base=0,
                                    pattern=[[-1, P]], channel_multiplier=1).then_inc(s_ident, 1)
            pool.wait_ge(d_bn, 96)
            nc.gpsimd.tensor_copy(pbd[:].rearrange("p q a r -> p a q r"), nbd[:].rearrange("p a (q r) -> p a q r", r=RK)).then_inc(s_perm, 1)
            nc.gpsimd.tensor_copy(pb1[:].rearrange("p q a r -> p a q r"), nb1[:].rearrange("p a (q r) -> p a q r", r=RK)).then_inc(s_perm, 1)
            pool.wait_ge(s_zero, 3)
            pool.wait_ge(s_ident, 2)

            def low(dst, src, high, s):
                nc.gpsimd.tensor_tensor(dst, src, f(high), ALU.subtract).then_inc(s, 1)

            def ring_low(u, g):
                ring_loaded(pool, u, g)
                pool.wait_ge(s_rh[u], ring_count(u, g))
                src, h, l = ring_views(u)
                low(l, src, h, s_rl[u])

            def x_low(n):
                pool.wait_ge(s_xh, n + 1)
                low(xsl[:], xraw[:], xsh[:], s_xl)

            def w0_plus(n):
                pool.wait_ge(d_w0, 64 * (n + 1))
                seen(pool, s_w0l, n)
                nc.gpsimd.tensor_tensor(w0i[:], w0raw[:], ident[:], ALU.add).then_inc(s_w0i, 1)

            def w0_low(n):
                pool.wait_ge(s_w0i, n + 1)
                pool.wait_ge(s_w0h, n + 1)
                low(w0l[:], w0i[:], w0h[:], s_w0l)

            def gathered_low(dst, raw, s_high, s_low, n):
                pool.wait_ge(s_high, n + 1)
                high, lo = parts(dst)
                nc.gpsimd.tensor_tensor(lo, raw[:].rearrange("p b (k r) -> p k b r", r=RK), f(high),
                                        ALU.subtract).then_inc(s_low, 1)

            w0_plus(0)
            x_low(0)
            w0_low(0)
            gathered_low(ag1, ag1r, s_ag1h, s_ag1l, 0)
            ring_low("bg1", -1)
            gathered_low(agu, agur, s_aguh, s_agul, 0)

            def step(g, prev, nxt):
                ring_low("gate0", g)
                ring_low("up0", g)
                ring_low("gate1", g)
                ring_low("up1", g)
                if nxt:
                    w0_plus(g + 1)
                ring_low("gate2", g)
                if nxt:
                    w0_low(g + 1)
                    x_low(g + 1)
                gathered_low(agd, agdr, s_agdh, s_agdl, g)
                ring_low("up2", g)
                if nxt:
                    gathered_low(ag1, ag1r, s_ag1h, s_ag1l, g + 1)
                    ring_low("bg1", g)
                    gathered_low(agu, agur, s_aguh, s_agul, g + 1)
                ring_low("bgd", g)

            loop(pool, step)

        @block.scalar
        def _(act):
            act.wait_ge(s_zero, 3)
            for half in range(2):
                q = slice(HID * half, HID * half + HID)
                act.dma_start(w2raw[q, HID + CH * half:HID + CH * half + CH], W2).then_inc(d_small, 16)
                act.dma_start(b3t[q, :], b3.rearrange("a h -> h a")).then_inc(d_small, 16)
            for b in range(NBG):
                act.dma_start(b2col[CH * b:CH * b + CH, :], b2.rearrange("(s o) -> s o", o=1)).then_inc(d_small, 16)
            for dst, src in ((bci, c3), (bcc, chans), (bcs, seqlen)):
                act.dma_start(dst[:], src.partition_broadcast(P)).then_inc(d_small, 16)
            act.wait_ge(d_bn, 96)
            nc.scalar.copy(pbu[:].rearrange("p q a r -> p a q r"), nbu[:].rearrange("p a (q r) -> p a q r", r=RK)).then_inc(s_perm, 1)
            for u in range(11):
                act.wait_ge(s_ta, u + 1)
                src = bank[4 + u % 4]
                if u == 0:
                    last = nc.scalar.copy(tab1[:].rearrange("p a (k r) -> p k a r", r=RK),
                                          src[:].rearrange("p (k a r) -> p k a r", k=KH, r=RK))
                elif u < 5:
                    which, s = (u - 1) // 2, (u - 1) % 2
                    dst = tab2[:, 8 * s:8 * s + 8, which * KH * RK:(which + 1) * KH * RK]
                    last = nc.scalar.copy(dst.rearrange("p a (k r) -> p k a r", r=RK),
                                          src[:].rearrange("p (k a r) -> p k a r", k=KH, r=RK))
                else:
                    s, j = (u - 5) // 3, (u - 5) % 3
                    full = 4 if j < 2 else 2
                    c = 4 * j
                    dst = tab2[:, 8 * s:8 * s + 8, AGU + c * RK:AGU + (c + full) * RK]
                    last = nc.scalar.copy(dst.rearrange("p a (k r) -> p k a r", r=RK),
                                          src[:, 0:full * P].rearrange("p (k a r) -> p k a r", k=full, r=RK))
                    if j == 2:
                        c = FC - 1
                        last = nc.scalar.copy(tab2[0:FLAST, 8 * s:8 * s + 8, AGU + c * RK:AGU + (c + 1) * RK],
                                              src[0:FLAST, 2 * P:3 * P].rearrange("p (a r) -> p a r", r=RK))
                last.then_inc(s_ea, 1)
            act.wait_ge(d_small, 16 * 15)
            nc.scalar.copy(w2h[:], w2raw[:]).then_inc(s_w2h, 1)
            act.wait_ge(d_scr, 80)
            for w in range(35):
                act.wait_ge(s_tw, w + 1)
                if w == 0:
                    act.wait_ge(s_const, 1)
                dst, src = weight_out(w, 0)
                nc.scalar.copy(dst, src).then_inc(s_wh, 1)

            def copy(dst, src, s):
                nc.scalar.activation(dst, src, ACT.Copy).then_inc(s, 1)

            def ring_high(u, g):
                ring_loaded(act, u, g)
                ring_free(act, u, g)
                src, h, _ = ring_views(u)
                copy(h, src, s_rh[u])

            def x_high(n):
                act.wait_ge(d_x, 16 * (n + 1))
                if isinstance(n, int) and n <= 1:
                    seen(act, s_l0, n)
                else:
                    act.wait_ge(s_h[1], n - 1)
                copy(xsh[:], xraw[:], s_xh)

            def w0_high(n):
                act.wait_ge(s_w0i, n + 1)
                seen(act, s_l0, n)
                copy(w0h[:], w0i[:], s_w0h)

            def gathered_high(dst, raw, d, used, s, n):
                act.wait_ge(d, 64 * (n + 1))
                seen(act, used, n)
                copy(parts(dst)[0], raw[:].rearrange("p b (k r) -> p k b r", r=RK), s)

            def stack_high(c, k, alone=False):
                act.wait_ge(s_tt[c], k + 1)
                stack_before(act, c, k, alone)
                n = ts[c].shape[1]
                copy(hh[:, 0:n], TURNED[c], s_hh[c])

            def x1_high(n):
                act.wait_ge(s_tx1, n + 1)
                copy(x1h, X[:], s_x1h)

            def x2_high(n):
                act.wait_ge(s_tx2, n + 1)
                copy(x2h[:], X[:], s_x2h)

            x_high(0)
            w0_high(0)
            gathered_high(ag1, ag1r, d_ag1, s_l1a, s_ag1h, 0)
            ring_loaded(act, "bg1", -1)
            _src, _h, _ = ring_views("bg1")
            copy(_h, _src, s_rh["bg1"])
            gathered_high(agu, agur, d_agu, s_ga, s_aguh, 0)
            x1_high(0)
            stack_high("t1", 0)
            x2_high(0)

            def silu(j, g):
                act.wait_ge(s_gate[j], g + 1)
                if j:
                    act.wait_ge(s_tr[j - 1], g + 1)
                else:
                    seen(act, s_tr[2], g)
                n = BLOCKS[j][1]
                nc.scalar.activation(sil[:, 0:n], GATE[j][:, 0:n], ACT.Silu).then_inc(s_sil[j], 1)

            def act_high(j, g):
                act.wait_ge(s_tr[j], g + 1)
                if j == 2:
                    act.wait_ge(s_dn[0], g + 1)
                else:
                    seen(act, s_dn[2 if j == 0 else 1], g)
                nf = -(-BLOCKS[j][1] // P) * P
                if j == 2:
                    nc.scalar.activation(ath[:, 0, 0:2 * P], TP[:, 0:2 * P], ACT.Copy)
                    copy(ath[0:FLAST, 0, 2 * P:3 * P], TP[0:FLAST, 2 * P:3 * P], s_ath[j])
                else:
                    copy(ath[:, j, 0:nf], TP[:, 0:nf], s_ath[j])

            def gelu(half, g):
                act.wait_ge(s_h[half], g + 1)
                seen(act, s_f3, g)
                nc.scalar.activation(graw[:, half, :], HB[half][:], ACT.Gelu,
                                     bias=cols[:, 2 + half:3 + half]).then_inc(s_gelu[half], 1)

            def gelu_high(half, g):
                act.wait_ge(s_gelu[half], g + 1)
                seen(act, s_o, g)
                copy(gh[:, half, :], graw[:, half, :], s_gh[half])

            def last_layer_a(g):
                gelu(0, g)
                gelu(1, g)
                gelu_high(0, g)
                gelu_high(1, g)

            def last_layer_b(g):
                act.wait_ge(s_o, g + 1)
                act.wait_ge(s_gl[0], g + 1)
                nc.scalar.activation(graw[:, 0, :], M[:], ACT.Identity, bias=b2col[:, 0:1]).then_inc(s_f1, 1)

            def w3_high(g):
                act.wait_ge(d_w3, 64 * (g + 1))
                act.wait_ge(s_meta, g + 1)
                seen(act, s_h[1], g)
                nc.scalar.activation(w3h[:], w3raw[:], ACT.Copy, scale=cols[:, 0:1]).then_inc(s_w3h, 1)

            def x3_high(g, last):
                act.wait_ge(s_x3r, g + 1)
                act.wait_ge(s_l0, g + 1 if last else g + 2)
                copy(xsh[:], x3raw[:], s_x3h)

            def step(g, prev, nxt):
                ring_high("gate0", g)
                stack_high("gu", g, not prev)
                ring_high("up0", g)
                if prev:
                    x3_high(g - 1, False)
                silu(0, g)
                ring_high("gate1", g)
                ring_high("up1", g)
                if prev:
                    last_layer_a(g - 1)
                ring_high("gate2", g)
                if nxt:
                    w0_high(g + 1)
                    x_high(g + 1)
                if prev:
                    nc.scalar.activation(scrap[:], colf[:, 0:1], ACT.Silu)
                silu(1, g)
                gathered_high(agd, agdr, d_agd, s_dn[2], s_agdh, g)
                ring_high("up2", g)
                if nxt:
                    gathered_high(ag1, ag1r, d_ag1, s_l1a, s_ag1h, g + 1)
                act_high(0, g)
                if prev:
                    last_layer_b(g - 1)
                silu(2, g)
                if nxt:
                    ring_high("bg1", g)
                    gathered_high(agu, agur, d_agu, s_ga, s_aguh, g + 1)
                act_high(1, g)
                if nxt:
                    x1_high(g + 1)
                ring_high("bgd", g)
                if nxt:
                    stack_high("t1", g + 1)
                act_high(2, g)
                if nxt:
                    x2_high(g + 1)
                w3_high(g)
                stack_high("td", g, not nxt)

            loop(act, step)
            x3_high(G - 1, True)
            last_layer_a(G - 1)
            last_layer_b(G - 1)

        @block.vector
        def _(dve):
            chain = [0]

            def link(ins):
                chain[0] += 1
                ins.then_inc(s_chain, 1)
                dve.wait_ge(s_chain, chain[0])

            link(nc.vector.memset(tab2[FLAST:P, :, AGU + AGD - RK:AGU + AGD], 0.0))
            link(nc.vector.memset(mask[:], 0.0))
            for b in range(NBG):
                q = slice(CH * b, CH * b + CH)
                link(nc.vector.memset(mask[q, q], 1.0))
            dve.wait_ge(s_iota, 2)
            dve.wait_ge(s_ident, 2)
            link(nc.vector.tensor_scalar(pidx[:, 1:2], pidx[:, 0:1], CH - 1, None, ALU.bitwise_and))
            link(nc.vector.tensor_scalar(pidx[:, 2:3], pidx[:, 0:1], 4, 1, ALU.logical_shift_right, ALU.bitwise_and))
            link(nc.vector.tensor_copy(colf[:, 0:2], pidx[:, 1:3]))
            link(nc.vector.tensor_scalar(colf[:, 2:3], colf[:, 1:2], -2.0, 1.0, ALU.mult, ALU.add))
            dve.wait_ge(d_bn, 96)
            nc.vector.tensor_copy(pbg[:].rearrange("p q a r -> p a q r"), nbg[:].rearrange("p a (q r) -> p a q r", r=RK)).then_inc(s_perm, 1)
            for u in range(19):
                dve.wait_ge(s_tb, u + 1)
                src = bank[u % 4]
                if u < 16:
                    t, s, q = u // 8, (u // 4) % 2, u % 4
                    dst = rows2[:, s, t * F:(t + 1) * F].rearrange("p (m q i) -> p q i m", q=4, i=4)[:, q]
                    last = nc.vector.tensor_copy(dst, src[:, 0:4 * FP].rearrange("p (i m) -> p i m", i=4))
                elif u < 18:
                    dst = rows2[:, u - 16, 2 * F:BROW].rearrange("p (m i) -> p i m", i=KH)
                    last = nc.vector.tensor_copy(dst, src[:].rearrange("p (i m) -> p i m", i=KH))
                else:
                    last = nc.vector.tensor_copy(rows1[:].rearrange("p (m i) -> p i m", i=KH),
                                                 src[:].rearrange("p (i m) -> p i m", i=KH))
                last.then_inc(s_eb, 1)
            dve.wait_ge(d_small, 16 * 15)
            for b in range(NBG):
                q = slice(CH * b, CH * b + CH)
                link(nc.vector.tensor_scalar(meta[q, :, 0], bcc[q, :].rearrange("p (g b) -> p b g", b=NBG)[:, b],
                                             colf[q, 0:1], None, ALU.is_gt))
                link(nc.vector.tensor_copy(meta[q, :, 1], bcs[q, :].rearrange("p (g b) -> p b g", b=NBG)[:, b]))
            for half in range(2):
                q = slice(HID * half, HID * half + HID)
                which = bci[q, :].rearrange("p (g s b) -> p b g s", s=2, b=2)[:, half]
                for a in range(NS):
                    dst = btmp[q] if a else meta[q, :, 2:4]
                    link(nc.vector.tensor_scalar(dst, which, float(a), b3t[q, a:a + 1], ALU.is_equal, ALU.mult))
                    if a:
                        link(nc.vector.tensor_tensor(meta[q, :, 2:4], meta[q, :, 2:4], btmp[q], ALU.add))
            nc.vector.tensor_copy(cols[:], meta[:, 0, :]).then_inc(s_const, 1)
            dve.wait_ge(s_w2h, 1)
            link(nc.vector.tensor_tensor(w2l[:], w2raw[:], f(w2h[:]), ALU.subtract))
            for w in range(35):
                dve.wait_ge(s_wh, w + 1)
                dst, src = weight_out(w, 1)
                high, _ = weight_out(w, 0)
                nc.vector.tensor_tensor(dst, src, f(high), ALU.subtract).then_inc(s_wl, 1)

            def low(dst, src, high, s):
                nc.vector.tensor_tensor(dst, src, f(high), ALU.subtract).then_inc(s, 1)

            def add_parts(c, scale, k, product, before, count, free, times):
                dve.wait_ge(product, k + 1)
                seen(dve, s_sum[before], count)
                n = ts[c].shape[1]
                w = n // P
                nc.vector.scalar_tensor_tensor(
                    out=tm[:, 0:n].rearrange("p (w n) -> p w n", w=w), in0=COEF[c].rearrange("p (w n) -> p w n", w=w),
                    scalar=scale, in1=mask[:].unsqueeze(1).broadcast_to([P, w, P]),
                    op0=ALU.mult, op1=ALU.mult).then_inc(s_tm[c], 1)
                dve.wait_ge(s_tm[c], k + 1)
                seen(dve, s_tt[free], times)
                v = tm[:, 0:n].rearrange("p (b c r) -> p b c r", c=2, r=RK)
                q = [v[:, :, i:i + 1, :].broadcast_to([P, w * NBG, 2, RK]) for i in range(2)]
                nc.vector.tensor_tensor(tsum[c][:].rearrange("p (b c r) -> p b c r", c=2, r=RK), q[0], q[1],
                                        ALU.add).then_inc(s_sum[c], 1)

            def stack(c, k, alone=False):
                dve.wait_ge(s_hh[c], k + 1)
                stack_before(dve, c, k, alone)
                n = ts[c].shape[1]
                nc.vector.tensor_scalar(tms[:, 0:n], TURNED[c], colf[:, 1:2], None, ALU.mult).then_inc(s_tms[c], 1)
                dve.wait_ge(s_tms[c], k + 1)
                nc.vector.scalar_tensor_tensor(out=ts[c][:], in0=f(hh[:, 0:n]), scalar=colf[:, 2:3], in1=tms[:, 0:n],
                                               op0=ALU.mult, op1=ALU.add).then_inc(s_ts[c], 1)

            def add_t1(n):
                add_parts("t1", 1.0, n, s_l1a, "gu", n, "td", max(n - 1, 0) if isinstance(n, int) else n - 1)

            def stack_t1(n):
                if not (isinstance(n, int) and n < 2):
                    dve.wait_ge(s_x3, n - 1)
                stack("t1", n)

            def add_td(g, last):
                if last:
                    add_parts("td", 0.5, g, s_dn[2], "gu", g + 1, "td", g)
                else:
                    add_parts("td", 0.5, g, s_dn[2], "t1", g + 2, "t1", g + 2)

            def stack_td(g, last):
                dve.wait_ge(s_l1b, g + 1 if last else g + 2)
                stack("td", g, last)

            def add_gu(n, first):
                add_parts("gu", 0.5, n, s_ga, "t1" if first else "td", 1 if first else n, "gu", n)

            def stack_gu(n, first):
                seen(dve, s_up[2], n)
                stack("gu", n, first)

            def x1_row(n):
                dve.wait_ge(s_l0, n + 1)
                if not (isinstance(n, int) and n < 2):
                    dve.wait_ge(s_f3, n - 1)
                nc.vector.tensor_copy(x1row, R[:]).then_inc(s_x1r, 1)

            def x1_low(n):
                dve.wait_ge(s_x1h, n + 1)
                low(x1l, X[:], x1h, s_x1l)

            def x2_row(n):
                dve.wait_ge(s_l1b, n + 1)
                seen(dve, s_pre, n)
                nc.vector.tensor_copy(x2row[:], R[:]).then_inc(s_x2r, 1)

            def x2_low(n):
                dve.wait_ge(s_x2h, n + 1)
                low(x2l[:], X[:], x2h[:], s_x2l)

            def keep_x2(g):
                seen(dve, d_out, g * 16)
                nc.vector.tensor_copy(x3raw[:], x2row[:]).then_inc(s_pre, 1)

            x1_row(0)
            x1_low(0)
            add_t1(0)
            stack_t1(0)
            x2_row(0)
            x2_low(0)
            add_gu(0, True)

            def mul(j, g):
                dve.wait_ge(s_sil[j], g + 1)
                dve.wait_ge(s_up[j], g + 1)
                n = BLOCKS[j][1]
                nc.vector.tensor_tensor(sil[:, 0:n], UP[j][:, 0:n], sil[:, 0:n], ALU.mult).then_inc(s_mul[j], 1)

            def act_low(j, g):
                dve.wait_ge(s_ath[j], g + 1)
                if j == 2:
                    nc.vector.tensor_tensor(atl[:, 0, 0:2 * P], TP[:, 0:2 * P], f(ath[:, 0, 0:2 * P]), ALU.subtract)
                    low(atl[0:FLAST, 0, 2 * P:3 * P], TP[0:FLAST, 2 * P:3 * P], ath[0:FLAST, 0, 2 * P:3 * P], s_atl[j])
                else:
                    low(atl[:, j, :], TP[:], ath[:, j, :], s_atl[j])

            def gelu_low(g):
                for half in range(2):
                    dve.wait_ge(s_gh[half], g + 1)
                    low(gl[:, half, :], graw[:, half, :], gh[:, half, :], s_gl[half])

            def finish(g):
                dve.wait_ge(s_f1, g + 1)
                nc.vector.scalar_tensor_tensor(out=graw[:, 1, :], in0=iota_t[:], scalar=cols[:, 1:2], in1=graw[:, 0, :],
                                               op0=ALU.is_lt, op1=ALU.mult).then_inc(s_f2, 1)
                dve.wait_ge(s_f2, g + 1)
                nc.vector.tensor_tensor(x3raw[:], x3raw[:], graw[:, 1, :], ALU.add).then_inc(s_f3, 1)

            def next_cols(g):
                if isinstance(g, int) and g == 0:
                    dve.wait_ge(s_const, 1)
                nc.vector.tensor_copy(cols[:], meta[:, bass.ds(g, 1), :].rearrange("p g c -> p (g c)")).then_inc(s_meta, 1)

            def x3_row(g):
                dve.wait_ge(s_x3, g + 1)
                dve.wait_ge(s_pre, g + 1)
                nc.vector.tensor_tensor(x3raw[:, 0:HALF], D[:, 0:HALF], x3raw[:, 0:HALF], ALU.add)
                nc.vector.tensor_tensor(x3raw[:, HALF:T], M[:, 0:HALF], x3raw[:, HALF:T], ALU.add).then_inc(s_x3r, 1)
                dve.wait_ge(s_x3h, g + 1)
                low(xsl[:], x3raw[:], xsh[:], s_x3l)

            def step(g, prev, nxt):
                stack_gu(g, not prev)
                if prev:
                    x3_row(g - 1)
                mul(0, g)
                if prev:
                    gelu_low(g - 1)
                mul(1, g)
                act_low(0, g)
                if prev:
                    finish(g - 1)
                next_cols(g)
                if nxt:
                    x1_row(g + 1)
                mul(2, g)
                act_low(1, g)
                if nxt:
                    x1_low(g + 1)
                if nxt:
                    add_t1(g + 1)
                    stack_t1(g + 1)
                act_low(2, g)
                keep_x2(g)
                if nxt:
                    x2_row(g + 1)
                    x2_low(g + 1)
                dve.wait_ge(s_w3h, g + 1)
                nc.vector.scalar_tensor_tensor(out=w3l[:], in0=w3raw[:], scalar=cols[:, 0:1], in1=f(w3h[:]),
                                               op0=ALU.mult, op1=ALU.subtract).then_inc(s_w3l, 1)
                add_td(g, not nxt)
                if nxt:
                    add_gu(g + 1, False)
                stack_td(g, not nxt)

            loop(dve, step)
            x3_row(G - 1)
            gelu_low(G - 1)
            finish(G - 1)

        @block.tensor
        def _(pe):
            pe.wait_ge(s_ident, 2)

            def tr(dst, src, n):
                return nc.tensor.transpose(dst, src, ident[0:n, 0:n])

            def b_unit(u):
                if u == 0:
                    pe.wait_ge(s_perm, 4)
                if u >= 4:
                    pe.wait_ge(s_eb, u - 3)
                dst = bank[u % 4]
                for i in range(4):
                    if u < 16:
                        t, s, q = u // 8, (u // 4) % 2, u % 4
                        src = (pbg, pbu)[t][:, 4 * q + i, 8 * s:8 * s + 8, :].rearrange("p a r -> p (a r)")
                        last = tr(dst[:, i * FP:(i + 1) * FP], src, FP)
                    else:
                        src = pbd[:, i, 8 * (u - 16):8 * (u - 16) + 8, :] if u < 18 else pb1[:, i]
                        last = tr(dst[:, i * P:(i + 1) * P], src.rearrange("p a r -> p (a r)"), P)
                last.then_inc(s_tb, 1)

            def a_unit(u):
                if u == 0:
                    pe.wait_ge(d_an, 64)
                if u >= 4:
                    pe.wait_ge(s_ea, u - 3)
                dst = bank[4 + u % 4]
                if u == 0:
                    pieces = [(na1[:, k * P:(k + 1) * P], P) for k in range(KH)]
                elif u < 5:
                    which, s = (u - 1) // 2, (u - 1) % 2
                    pieces = [((nag, nau)[which][:, s, k * P:(k + 1) * P], P) for k in range(KH)]
                else:
                    s, j = (u - 5) // 3, (u - 5) % 3
                    pieces = [(nad[:, s, c * P:min(F, (c + 1) * P)], min(P, F - c * P)) for c in range(4 * j, min(FC, 4 * j + 4))]
                for i, (src, m) in enumerate(pieces):
                    last = tr(dst[0:m, i * P:(i + 1) * P], src, P)
                last.then_inc(s_ta, 1)

            for u in range(19):
                b_unit(u)
                if u < 11:
                    a_unit(u)
            pe.wait_ge(s_ea, 11)
            pe.wait_ge(s_eb, 19)
            pe.wait_ge(d_wn, 64)
            for w in range(35):
                if w == 24:
                    pe.wait_ge(d_wn, 80)
                if w >= 8:
                    pe.wait_ge(s_wl, w - 7)
                dst = bank[w % 8]
                if w < 24:
                    t, k, j = w // 12, (w % 12) // 3, w % 3
                    for c in range(4 * j, min(FC, 4 * j + 4)):
                        m = min(P, F - c * P)
                        o = (c - 4 * j) * P
                        last = tr(dst[:, o:o + m], (nwg, nwu)[t][0:m, c, k * P:(k + 1) * P], m)
                else:
                    c = w - 24
                    m = min(P, F - c * P)
                    for k in range(KH):
                        last = tr(dst[0:m, k * P:(k + 1) * P], nwd[:, k, c * P:c * P + m], P)
                last.then_inc(s_tw, 1)

            def passes(dst, sh, sl, mh, ml, first, last_):
                nc.tensor.matmul(dst, sh, mh, start=first, stop=False)
                nc.tensor.matmul(dst, sl, mh, start=False, stop=False)
                return nc.tensor.matmul(dst, sh, ml, start=False, stop=last_)

            def turn(c, k):
                pe.wait_ge(s_sum[c], k + 1)
                for i in range(ts[c].shape[1] // P):
                    last = tr(TURNED[c][:, i * P:(i + 1) * P], tsum[c][:, i * P:(i + 1) * P], P)
                last.then_inc(s_tt[c], 1)

            def chunk(ap, k):
                return ap[:, k * P:(k + 1) * P]

            def layer0(n):
                pe.wait_ge(s_xl, n + 1)
                pe.wait_ge(s_w0l, n + 1)
                seen(pe, s_mul[1], n)
                passes(R[:], w0h[:], w0l[:], xsh[:], xsl[:], True, True).then_inc(s_l0, 1)

            def turn_x(src, ready, done, n):
                pe.wait_ge(ready, n + 1)
                for k in range(KH):
                    last = tr(chunk(X, k), chunk(src, k), P)
                last.then_inc(done, 1)

            def turn_x1(n):
                seen(pe, s_x2l, n)
                turn_x(x1row, s_x1r, s_tx1, n)

            def turn_x2(n):
                turn_x(x2row, s_x2r, s_tx2, n)

            def layer1_a(n):
                pe.wait_ge(s_x1l, n + 1)
                pe.wait_ge(s_ag1l, n + 1)
                for k in range(KH):
                    nc.tensor.matmul(COEF["t1"], chunk(x1h, k), ag1[:, k, :], start=(k == 0), stop=False)
                    last = nc.tensor.matmul(COEF["t1"], chunk(x1l, k), ag1[:, k, :], start=False, stop=(k == KH - 1))
                last.then_inc(s_l1a, 1)

            def rank_b(dst, stat, u, n, o=0, check=True):
                i = RING.index(u) % 2
                nc.tensor.matmul(dst, stat, ringh[:, i, o:o + n], start=False, stop=False, skip_group_check=not check)
                return nc.tensor.matmul(dst, stat, ringl[:, i, o:o + n], start=False, stop=True, skip_group_check=not check)

            def layer1_b(n):
                pe.wait_ge(s_ts["t1"], n + 1)
                pe.wait_ge(s_rl["bg1"], n + 1)
                rank_b(R[:], ts_x[:], "bg1", T, check=False).then_inc(s_l1b, 1)

            def rank_gu_a(n):
                pe.wait_ge(s_x2l, n + 1)
                pe.wait_ge(s_agul, n + 1)
                for k in range(KH):
                    both = agu[:].rearrange("p (w k) n -> p k w n", w=2)[:, k]
                    nc.tensor.matmul(COEF["gu"], chunk(x2h, k), both, start=(k == 0), stop=False)
                    last = nc.tensor.matmul(COEF["gu"], chunk(x2l, k), both, start=False, stop=(k == KH - 1))
                last.then_inc(s_ga, 1)

            def dense(which, j):
                f0, n = BLOCKS[j]
                dst, o = (GATE, UP)[which][j], which * F + f0
                for k in range(KH):
                    passes(dst[:, 0:n], chunk(x2h, k), chunk(x2l, k), wguh[:, k, o:o + n], wgul[:, k, o:o + n],
                           k == 0, False)

            def rank_gu_b(which, j, g):
                n = BLOCKS[j][1]
                pe.wait_ge(s_ts["gu"], g + 1)
                u = ("gate", "up")[which] + str(j)
                pe.wait_ge(s_rl[u], g + 1)
                rank_b((GATE, UP)[which][j][:, 0:n], ts_gu[:, which * P:(which + 1) * P], u, n) \
                    .then_inc((s_gate, s_up)[which][j], 1)

            def transpose_act(j, g):
                pe.wait_ge(s_mul[j], g + 1)
                if j:
                    pe.wait_ge(s_atl[j - 1], g + 1)
                else:
                    seen(pe, s_gelu[1], g)
                for i in range(-(-BLOCKS[j][1] // P)):
                    m = min(P, BLOCKS[j][1] - i * P)
                    last = tr(TP[0:m, i * P:(i + 1) * P], sil[:, i * P:i * P + m], P)
                last.then_inc(s_tr[j], 1)

            def down(c, g):
                j, i = c // 4, c % 4
                if c == 0:
                    pe.wait_ge(s_agdl, g + 1)
                    seen(pe, s_gelu[0], g)
                    seen(pe, s_f1, g)
                if i == 0:
                    pe.wait_ge(s_atl[j], g + 1)
                m = min(P, F - c * P)
                h, l = (a[0:m, j % 2, i * P:(i + 1) * P] for a in (ath, atl))
                end = c == FC - 1
                first = c == 0
                if end:
                    nc.tensor.matmul(M[:, 0:HALF], h, wdl[0:m, c, HALF:T], start=False, stop=False, skip_group_check=True)
                nc.tensor.matmul(D[:, 0:HALF], h, wdh[0:m, c, 0:HALF], start=first, stop=False)
                nc.tensor.matmul(M[:, 0:HALF + P], h, wdh[0:m, c, HALF:T + P], start=first, stop=False)
                nc.tensor.matmul(D[:, 0:HALF], h, wdl[0:m, c, 0:HALF], start=False, stop=False)
                if not end:
                    nc.tensor.matmul(M[:, 0:HALF], h, wdl[0:m, c, HALF:T], start=False, stop=False)
                nc.tensor.matmul(D[:, 0:HALF], l, wdh[0:m, c, 0:HALF], start=False, stop=end)
                last = nc.tensor.matmul(M[:, 0:HALF + P], l, wdh[0:m, c, HALF:T + P], start=False, stop=end)
                if i == 3 or end:
                    last.then_inc(s_dn[j], 1)

            def rank_down_b(g):
                pe.wait_ge(s_ts["td"], g + 1)
                pe.wait_ge(s_rl["bgd"], g + 1)
                rank_b(D[:, 0:HALF], ts_x[:], "bgd", HALF, 0, check=False)
                rank_b(M[:, 0:HALF], ts_x[:], "bgd", HALF, HALF, check=False).then_inc(s_x3, 1)

            def layer3_a(g):
                pe.wait_ge(s_x3l, g + 1)
                pe.wait_ge(s_w3l, g + 1)
                for half in range(2):
                    passes(HB[half][:], chunk(w3h, half), chunk(w3l, half), xsh[:], xsl[:], True, True) \
                        .then_inc(s_h[half], 1)

            def layer3_b(g):
                for half in range(2):
                    pe.wait_ge(s_gl[half], g + 1)
                    o = HID * (1 - half)
                    last = passes(M[:], w2h[:, o:o + P], w2l[:, o:o + P], gh[:, half, :], gl[:, half, :], half == 0, half == 1)
                last.then_inc(s_o, 1)

            pe.wait_ge(s_wl, 35)
            layer0(0)
            turn_x1(0)
            layer1_a(0)
            turn("t1", 0)
            layer1_b(0)
            turn_x2(0)
            rank_gu_a(0)

            def step(g, prev, nxt):
                seen(pe, s_mul[2], g)
                dense(0, 0)
                turn("gu", g)
                if prev:
                    rank_down_b(g - 1)
                dense(1, 0)
                rank_gu_b(0, 0, g)
                rank_gu_b(1, 0, g)
                if prev:
                    layer3_a(g - 1)
                dense(0, 1)
                rank_gu_b(0, 1, g)
                dense(1, 1)
                rank_gu_b(1, 1, g)
                transpose_act(0, g)
                if prev:
                    layer3_b(g - 1)
                pe.wait_ge(s_mul[0], g + 1)
                dense(0, 2)
                rank_gu_b(0, 2, g)
                if nxt:
                    layer0(g + 1)
                transpose_act(1, g)
                dense(1, 2)
                rank_gu_b(1, 2, g)
                if nxt:
                    turn_x1(g + 1)
                for c in range(FC):
                    down(c, g)
                    if c == 2 and nxt:
                        layer1_a(g + 1)
                    if c == 3 and nxt:
                        turn("t1", g + 1)
                    if c == 3:
                        transpose_act(2, g)
                    if c == 5 and nxt:
                        layer1_b(g + 1)
                    if c == 7 and nxt:
                        turn_x2(g + 1)
                if nxt:
                    rank_gu_a(g + 1)
                turn("td", g)

            loop(pe, step)
            rank_down_b(G - 1)
            layer3_a(G - 1)
            layer3_b(G - 1)


_INS = ["x", "itok_B_0_15", "itok_B_3_7", "itok_B_2_6", "itok_B_0_7", "itok_B_2182_4065", "_lenS",
        "L0_cond_weights", "L1_cond_A", "L1_cond_B", "L2_cond_W_gate", "L2_cond_W_up", "L2_cond_W_down",
        "L2_cond_A_gate", "L2_cond_B_gate", "L2_cond_A_up", "L2_cond_B_up", "L2_cond_A_down",
        "L2_cond_B_down", "L3_cond_W_sess", "L3_cond_b_sess", "L3_cond_W2", "L3_cond_b2"]


def kernel(**inputs):
    import numpy as _np
    import concourse.bass as _bass
    import concourse.bacc as _bacc
    from concourse import mybir as _mybir
    from concourse.bass_utils import run_bass_kernel_spmd as _run

    nc = _bacc.Bacc("TRN2", target_bir_lowering=False, num_devices=1, dynamic_dma_scratch_size=1024)
    arrays, args = {}, []
    for name in _INS:
        a = _np.ascontiguousarray(inputs[name])
        arrays[f"in_{name}_dram"] = a
        args.append(nc.dram_tensor(f"in_{name}_dram", a.shape, _mybir.dt.from_np(a.dtype), kind="ExternalInput").ap())
    out = nc.dram_tensor("out_0_dram", (BATCH, CH, T), _mybir.dt.float32, kind="ExternalOutput").ap()
    build(nc, _bass, _mybir, *args, out)
    r = _run(nc, [arrays], core_ids=[0])
    return r.results[0]["out_0_dram"]
```

```python
BATCH, CH, T = 128, 32, 512
P = 128
NBG = P // CH
G = BATCH // NBG
AT_ONCE = 3
KH = T // P
F = 1376
FC = -(-F // P)
FLAST = F - (FC - 1) * P
RK = 16
NA1, NA2, NS = 8, 16, 8
HID = 64
BLOCKS = [(0, 512), (512, 512), (1024, F - 1024)]
BROW = 2 * F + T
AGU, AGD = 2 * KH * RK, FC * RK
WGU, WALL = 2 * KH * len(BLOCKS), 2 * KH * len(BLOCKS) + FC
FQ = 16
FP = F // FQ


def build(nc, bass, mybir, x, c0, c1, c2, c3, seqlen, chans, W0, A1, B1, Wg, Wu, Wd, Ag, Bg, Au, Bu,
          Ad, Bd, W3, b3, W2, b2, out):
    from contextlib import ExitStack

    F32, R32, I32, I16 = mybir.dt.float32, mybir.dt.float32r, mybir.dt.int32, mybir.dt.int16
    ALU, ACT = mybir.AluOpType, mybir.ActivationFunctionType
    ctx = ExitStack()
    with ctx:
        ctx.enter_context(nc.allow_non_contiguous_dma(reason="small tables, once"))

        def sb(name, shape, dt):
            return ctx.enter_context(nc.sbuf_tensor(name, shape, dt))

        def sem(name):
            return ctx.enter_context(nc.semaphore(name))

        def f(ap):
            return ap.bitcast(F32)

        ident = sb("ident", [P, P], F32)
        mask = sb("mask", [P, P], F32)
        pidx = sb("pidx", [P, 4], I32)
        colf = sb("colf", [P, 4], F32)
        iota_t = sb("iota_t", [P, T], I16)
        meta = sb("meta", [P, G, 5], F32)
        cols = sb("cols", [P, 5], F32)
        scrap = sb("scrap", [P, 1], F32)
        b2col = sb("b2col", [P, 1], F32)
        idx = sb("idx", [4, BATCH], I32)
        w0raw = sb("w0raw", [P, P], F32)
        w0i = sb("w0i", [P, P], F32)
        w0h, w0l = sb("w0h", [P, P], R32), sb("w0l", [P, P], R32)
        w3raw = sb("w3raw", [P, NBG * HID], F32)
        w3h, w3l = sb("w3h", [P, NBG * HID], R32), sb("w3l", [P, NBG * HID], R32)
        w2h, w2l = sb("w2h", [P, 192], R32), sb("w2l", [P, 192], R32)

        at_w = nc.sbuf_base
        wguh, wgul = (sb(n, [P, KH, 2 * F], R32) for n in ("wguh", "wgul"))
        at_wd = nc.sbuf_base
        wdh, wdl = sb("wdh", [P, FC, T + P], R32), sb("wdl", [P, FC, T], R32)

        at_work = nc.sbuf_base
        x2h, x2l = sb("x2h", [P, T], R32), sb("x2l", [P, T], R32)
        x2row = sb("x2row", [P, T], F32)
        ag1r, ag1 = sb("ag1r", [P, NBG, KH * RK], F32), sb("ag1", [P, KH, P], R32)
        agur, agu = sb("agur", [P, NBG, AGU], F32), sb("agu", [P, 2 * KH, P], R32)
        bg1 = sb("bg1", [P, T], F32)
        ringh, ringl = (sb(n, [P, 2, 512], R32) for n in ("ringh", "ringl"))
        tm = sb("tm", [P, 2 * P], F32)
        tsum_x, tsum_gu = sb("tsum_x", [P, P], F32), sb("tsum_gu", [P, 2 * P], F32)
        tsum = {"t1": tsum_x, "td": tsum_x, "gu": tsum_gu}
        hh, tms = sb("hh", [P, 2 * P], R32), sb("tms", [P, 2 * P], F32)
        ts_x, ts_gu = sb("ts_x", [P, P], R32), sb("ts_gu", [P, 2 * P], R32)
        ts = {"t1": ts_x, "td": ts_x, "gu": ts_gu}
        sil = sb("sil", [P, 512], F32)
        bg2 = sb("bg2", [P, BROW], F32)
        at_x = nc.sbuf_base
        xraw = sb("xraw", [P, T], F32)
        xsh, xsl = sb("xsh", [P, T], R32), sb("xsl", [P, T], R32)
        x3s = (xsh, xsl)
        SIDE = P // 2
        at_late = nc.sbuf_base
        gh, gl = (sb(n, [P, 2, T], R32) for n in ("gh", "gl"))
        graw = sb("graw", [P, 2, T], F32)
        x1row, x1h, x1l = graw[:, 1, :], gh[:, 1, :], gl[:, 1, :]
        x3raw = sb("x3raw", [P, T], F32)
        ath, atl = (sb(n, [P, 2, 512], R32) for n in ("ath", "atl"))
        at_last = nc.sbuf_base
        agdr, agd = sb("agdr", [P, NBG, AGD], F32), wdh[:, :, T:T + P]

        def at(place):
            here = [place]

            def alloc(name, shape, dt):
                n = 4
                for s in shape[1:]:
                    n *= s
                t = nc.alloc_sbuf_tensor_at(name, shape, dt, offset=here[0])
                here[0] += -(-n // 32) * 32
                return t
            return alloc

        st = at(at_w)
        nbg, nbu = (st(n, [FP, NA2, FQ * RK], F32) for n in ("nbg", "nbu"))
        nbd = st("nbd", [P, NA2, KH * RK], F32)
        nb1 = st("nb1", [P, NA1, KH * RK], F32)
        nag, nau = (st(n, [P, 2, T], F32) for n in ("nag", "nau"))
        nad = st("nad", [P, 2, F], F32)
        na1 = st("na1", [P, T], F32)
        pbg = st("pbg", [FP, FQ, NA2, RK], F32)
        st = at(at_wd - 4096)
        bci, bcc, bcs = (st(n, [P, BATCH], I32) for n in ("bci", "bcc", "bcs"))
        b3t = st("b3t", [P, NS], F32)
        pair = st("pair", [P, G, 2], I32)
        btmp = st("btmp", [P, G, 2], F32)
        w2raw = st("w2raw", [P, 192], F32)
        st = at(at_wd)
        rows2 = st("rows2", [P, 2, BROW], F32)
        rows1 = st("rows1", [P, T], F32)
        tab2 = st("tab2", [P, NA2, AGU + AGD], F32)
        tab1 = st("tab1", [P, NA1, KH * RK], F32)
        st = at(at_work)
        nwg, nwu = (st(n, [P, FC, T], F32) for n in ("nwg", "nwu"))
        assert at_work + 2 * FC * T * 4 <= at_x
        nwd = at(at_late)("nwd", [P, KH, F], F32)
        assert at_late + KH * F * 4 <= at_last
        st = at(at_late)
        pbu = st("pbu", [FP, FQ, NA2, RK], F32)
        pbd = st("pbd", [P, KH, NA2, RK], F32)
        pb1 = st("pb1", [P, KH, NA1, RK], F32)

        scr_a1 = nc.dram_tensor("scr_a1", [NA1, P, KH * RK], F32, kind="Internal").ap()
        scr_a2 = nc.dram_tensor("scr_a2", [NA2, P, AGU + AGD], F32, kind="Internal").ap()
        scr_b1 = nc.dram_tensor("scr_b1", [NA1, RK, T], F32, kind="Internal").ap()
        scr_b2 = nc.dram_tensor("scr_b2", [NA2, RK, BROW], F32, kind="Internal").ap()

        bank = [ctx.enter_context(nc.psum_tensor(f"bank{i}", [P, 512], F32)) for i in range(8)]
        GATE = [bank[0], bank[2], bank[0]]
        UP = [bank[1], bank[3], bank[1]]
        X, TP, D, M = bank[4], bank[5], bank[6], bank[7]
        HB = [D, TP]
        R, C = bank[2], bank[3]
        HALF = T // 2
        COEF = {"t1": C[:, 0:P], "td": M[:, HALF:HALF + P], "gu": C[:, 0:2 * P]}
        TURNED = {"t1": C[:, P:2 * P], "td": TP[:, 0:P], "gu": C[:, 2 * P:4 * P]}

        d_small, d_tables, d_idx, d_an = sem("d_small"), sem("d_tables"), sem("d_idx"), sem("d_an")
        d_nbg, d_nbu, d_nbd, d_nb1 = (sem(f"d_{n}") for n in ("nbg", "nbu", "nbd", "nb1"))
        d_nwg, d_nwu, d_nwd = sem("d_nwg"), sem("d_nwu"), sem("d_nwd")
        d_scr, d_scr_b2 = sem("d_scr"), sem("d_scr_b2")
        d_x, d_w0, d_ag1, d_bg1, d_agu = (sem(f"d_{n}") for n in ("x", "w0", "ag1", "bg1", "agu"))
        d_bg2, d_agd, d_w3, d_out = (sem(f"d_{n}") for n in ("bg2", "agd", "w3", "out"))
        s_zero, s_iota, s_ident, s_chain, s_const = (sem(f"s_{n}") for n in ("zero", "iota", "ident", "chain", "const"))
        s_tb, s_eb, s_ta, s_ea, s_tw, s_wh, s_wl = (sem(f"s_{n}") for n in ("tb", "eb", "ta", "ea", "tw", "wh", "wl"))
        s_w2h = sem("s_w2h")
        s_pbg, s_pbu, s_pbd, s_pb1 = (sem(f"s_{n}") for n in ("pbg", "pbu", "pbd", "pb1"))
        s_xh, s_xl, s_w0i, s_w0h, s_w0l = (sem(f"s_{n}") for n in ("xh", "xl", "w0i", "w0h", "w0l"))
        s_ag1h, s_ag1l, s_aguh, s_agul, s_agdh, s_agdl = (sem(f"s_{n}") for n in ("ag1h", "ag1l", "aguh", "agul", "agdh", "agdl"))
        s_w3h, s_w3l, s_meta = sem("s_w3h"), sem("s_w3l"), sem("s_meta")
        RING = ["bgd", "gate0", "up0", "gate1", "up1", "gate2", "up2", "bg1"]
        s_rh = {u: sem(f"s_rh_{u}") for u in RING}
        s_rl = {u: sem(f"s_rl_{u}") for u in RING}
        s_l0, s_l1a, s_l1b, s_ga = (sem(f"s_{n}") for n in ("l0", "l1a", "l1b", "ga"))
        s_x1r, s_tx1, s_x2r, s_tx2, s_pre = (sem(f"s_{n}") for n in ("x1r", "tx1", "x2r", "tx2", "pre"))
        s_gate = [sem(f"s_gate{j}") for j in range(3)]
        s_up = [sem(f"s_up{j}") for j in range(3)]
        s_tr = [sem(f"s_tr{j}") for j in range(3)]
        s_dn = [sem(f"s_dn{j}") for j in range(3)]
        s_x3, s_o = sem("s_x3"), sem("s_o")
        s_h = [sem(f"s_h{j}") for j in range(2)]
        s_x1h, s_x1l, s_x2h, s_x2l = (sem(f"s_{n}") for n in ("x1h", "x1l", "x2h", "x2l"))
        s_tm, s_sum, s_tt, s_hh, s_tms, s_ts = ({c: sem(f"s_{n}_{c}") for c in ts}
                                                for n in ("tm", "sum", "tt", "hh", "tms", "ts"))
        s_sil = [sem(f"s_sil{j}") for j in range(3)]
        s_mul = [sem(f"s_mul{j}") for j in range(3)]
        s_ath = [sem(f"s_ath{j}") for j in range(3)]
        s_atl = [sem(f"s_atl{j}") for j in range(3)]
        s_x3r, s_x3h, s_x3l = sem("s_x3r"), sem("s_x3h"), sem("s_x3l")
        s_gelu = [sem(f"s_gelu{j}") for j in range(2)]
        s_gh = [sem(f"s_gh{j}") for j in range(2)]
        s_gl = [sem(f"s_gl{j}") for j in range(2)]
        s_f1, s_f2, s_f3 = sem("s_f1"), sem("s_f2"), sem("s_f3")

        def seen(eng, s, count):
            if not (isinstance(count, int) and count == 0):
                eng.wait_ge(s, count)

        ring_src = {"bg1": (bg1, 0, 512), "bgd": (bg2, 2 * F, 512)}
        for j, (f0, n) in enumerate(BLOCKS):
            ring_src[f"gate{j}"] = (bg2, f0, n)
            ring_src[f"up{j}"] = (bg2, F + f0, n)

        def ring_free(eng, u, g):
            if u == "bgd":
                eng.wait_ge(s_up[2], g + 1)
            elif u == "gate0":
                eng.wait_ge(s_l1b, g + 1)
            elif u == "up0":
                seen(eng, s_x3, g)
            elif u == "bg1":
                seen(eng, s_gate[2], g + 1)
            else:
                j = int(u[-1])
                eng.wait_ge((s_gate if u.startswith("gate") else s_up)[j - 1], g + 1)

        def ring_views(u):
            src, o, n = ring_src[u]
            i = RING.index(u) % 2
            return src[:, o:o + n], ringh[:, i, 0:n], ringl[:, i, 0:n]

        def ring_loaded(eng, u, g):
            if u == "bg1":
                eng.wait_ge(d_bg1, 64 * (g + 2))
            else:
                eng.wait_ge(d_bg2, 64 * (g + 1))

        def ring_count(u, g):
            return g + 2 if u == "bg1" else g + 1

        def loop(eng, step):
            step(0, False, True)
            assert (G - 2) % AT_ONCE == 0
            with eng.Fori(0, (G - 2) // AT_ONCE) as turn:
                for i in range(AT_ONCE):
                    step(turn * AT_ONCE + (i + 1), True, True)
            step(G - 1, True, False)

        DOWN_UNITS = [range(w, min(w + 3, WALL)) for w in range(WGU, WALL, 3)]

        def weight_bank(w):
            return bank[w % 8] if w < WGU else bank[(4, 6, 7)[(w - WGU) % 3]]

        def weight_out(w, low):
            src = weight_bank(w)
            if w < WGU:
                t, k, j = w // 12, (w % 12) // 3, w % 3
                f0, n = BLOCKS[j]
                return (wguh, wgul)[low][:, k, t * F + f0:t * F + f0 + n], src[:, 0:n]
            c = w - WGU
            n = P if c < FC - 1 else FLAST
            return (wdh, wdl)[low][0:n, c, 0:T], src[0:n, :]

        def parts(split):
            v = split[:].rearrange("p k (b c r) -> p c k b r", b=NBG, c=2)
            return v[:, 0], v[:, 1]

        def stack_before(eng, c, n, alone=False):
            if c == "t1":
                seen(eng, s_ts["gu"], n)
            elif c == "td":
                eng.wait_ge(s_ts["gu"], n + 1) if alone else eng.wait_ge(s_ts["t1"], n + 2)
            else:
                eng.wait_ge(s_ts["t1"], 1) if alone else eng.wait_ge(s_ts["td"], n)

        x_rows = x.rearrange("b c t -> (b c) t")
        out_rows = out.rearrange("b c t -> (b c) t")
        block = ctx.enter_context(nc.Block())

        @block.sync
        def _(sp):
            for dst, src, done in ((nbg, Bg, d_nbg), (nbu, Bu, d_nbu)):
                v = src[0].rearrange("a (p q) r -> p a (q r)", q=FQ)
                sp.dma_start(dst[0:80], v[0:80]).then_inc(done, 16)
                sp.dma_start(dst[80:FP], v[80:FP]).then_inc(done, 16)
            sp.dma_start(nbd[:], Bd[0].rearrange("a (p q) r -> p a (q r)", q=KH)).then_inc(d_nbd, 16)
            sp.dma_start(nb1[:], A1.rearrange("a (p q) r -> p a (q r)", q=KH)).then_inc(d_nb1, 16)
            sp.dma_start(na1[:], B1.rearrange("a r h -> (a r) h")).then_inc(d_an, 16)
            for dst, src in ((nag, Ag), (nau, Au), (nad, Ad)):
                sp.dma_start(dst[:], src[0].rearrange("(s a) r h -> (a r) s h", s=2)).then_inc(d_an, 16)
            for i, c in enumerate((c0, c1, c2, c3)):
                sp.dma_start(idx[i:i + 1, :], c.rearrange("(o b) -> o b", o=1)).then_inc(d_idx, 16)
            for dst, src, done in ((nwg, Wg, d_nwg), (nwu, Wu, d_nwu)):
                n = (FC - 1) * P
                sp.dma_start(dst[:, 0:FC - 1, :], src[0:n, :].rearrange("(c p) h -> p c h", p=P)).then_inc(done, 16)
                sp.dma_start(dst[0:FLAST, FC - 1, :], src[n:F, :]).then_inc(done, 16)
            sp.wait_ge(d_idx, 64)
            sp.wait_ge(s_zero, 3)

            def chosen(row, n, k):
                return [sp.value_load(idx[row:row + 1, bass.ds(NBG * n + b, 1)], min_val=0, max_val=k - 1)
                        for b in range(NBG)]

            def twice(rows):
                return rows.broadcast_to([2, RK, rows.shape[2]])

            def load_x(n):
                seen(sp, s_xh, n)
                seen(sp, s_xl, n)
                sp.dma_start(xraw[:], x_rows[bass.ds(n * P, P), :]).then_inc(d_x, 16)

            def load_w0(n):
                v = chosen(0, n, 16)
                seen(sp, s_w0i, n)
                for b in range(NBG):
                    q = slice(CH * b, CH * b + CH)
                    sp.dma_start(w0raw[q, q], W0[bass.ds(v[b], 1)].rearrange("a c d -> (a c) d")).then_inc(d_w0, 16)

            def load_rank1(n):
                v = chosen(1, n, NA1)
                seen(sp, s_ag1l, n)
                for b in range(NBG):
                    sp.dma_start(ag1r[:, b, :], scr_a1[bass.ds(v[b], 1)].rearrange("a p n -> (a p) n")).then_inc(d_ag1, 16)
                seen(sp, s_rl["bg1"], n)
                for b in range(NBG):
                    sp.dma_start(bg1[CH * b:CH * b + CH, :], twice(scr_b1[bass.ds(v[b], 1)])).then_inc(d_bg1, 16)

            def load_agu(v, n):
                seen(sp, s_agul, n)
                for b in range(NBG):
                    sp.dma_start(agur[:, b, :], scr_a2[bass.ds(v[b], 1), :, 0:AGU].rearrange("a p n -> (a p) n")).then_inc(d_agu, 16)

            def load_agd(v, n):
                seen(sp, s_agdl, n)
                for b in range(NBG):
                    sp.dma_start(agdr[:, b, :], scr_a2[bass.ds(v[b], 1), :, AGU:AGU + AGD].rearrange("a p n -> (a p) n")).then_inc(d_agd, 16)

            def load_bg2(v, n):
                seen(sp, s_rl["bgd"], n)
                for b in range(NBG):
                    sp.dma_start(bg2[CH * b:CH * b + CH, :], twice(scr_b2[bass.ds(v[b], 1)])).then_inc(d_bg2, 16)

            def load_w3(g):
                v = chosen(3, g, NS)
                seen(sp, s_w3l, g)
                for b in range(NBG):
                    for rows in (CH * b, (CH * b + P // 2) % P):
                        sp.dma_start(w3raw[rows:rows + CH, HID * b:HID * b + HID],
                                     W3[bass.ds(v[b], 1)].rearrange("a c d -> (a c) d")).then_inc(d_w3, 16)

            def store(g, count):
                sp.wait_ge(s_f3, count)
                sp.dma_start(out_rows[bass.ds(g * P, P), :], x3raw[:]).then_inc(d_out, 16)

            load_x(0)
            load_w0(0)
            sp.wait_ge(s_ea, 11)
            sp.dma_start(scr_a1.rearrange("a p n -> p a n"), tab1[:]).then_inc(d_scr, 16)
            sp.dma_start(scr_a2.rearrange("a p n -> p a n"), tab2[:]).then_inc(d_scr, 16)
            sp.wait_ge(s_eb, 19)
            sp.dma_start(scr_b1[:], rows1[:]).then_inc(d_scr, 16)
            sp.dma_start(scr_b2[0:8], rows2[:, 0, :]).then_inc(d_scr_b2, 16)
            sp.wait_ge(d_scr, 48)
            sp.wait_ge(s_tw, WGU)
            load_rank1(0)
            sp.dma_start(scr_b2[8:16], rows2[:, 1, :]).then_inc(d_scr_b2, 16)
            v0 = chosen(2, 0, NA2)
            load_agu(v0, 0)
            sp.wait_ge(d_scr_b2, 32)
            load_bg2(v0, 0)
            load_agd(v0, 0)
            sp.wait_ge(s_l1a, 1)
            sp.dma_start(nwd[:], Wd.rearrange("(c p) f -> p c f", p=P)).then_inc(d_nwd, 16)

            def step(g, prev, nxt):
                if nxt:
                    load_x(g + 1)
                    load_w0(g + 1)
                    load_rank1(g + 1)
                load_w3(g)
                if nxt:
                    v = chosen(2, g + 1, NA2)
                    load_agu(v, g + 1)
                    load_agd(v, g + 1)
                if prev:
                    store(g - 1, g)
                if nxt:
                    load_bg2(v, g + 1)

            loop(sp, step)
            store(G - 1, G)
            sp.wait_ge(d_out, 16 * G)

        @block.gpsimd
        def _(pool):
            nc.gpsimd.memset(w0raw[:], 0.0).then_inc(s_zero, 1)
            nc.gpsimd.memset(w3raw[:], 0.0).then_inc(s_zero, 1)
            nc.gpsimd.memset(w2raw[:], 0.0).then_inc(s_zero, 1)
            nc.gpsimd.iota(pidx[:, 0:1], pattern=[[0, 1]], base=0, channel_multiplier=1).then_inc(s_iota, 1)
            nc.gpsimd.iota(iota_t[:], pattern=[[1, T]], base=0, channel_multiplier=0).then_inc(s_iota, 1)
            nc.gpsimd.memset(ident[:], 0.0).then_inc(s_ident, 1)
            pool.wait_ge(s_ident, 1)
            nc.gpsimd.affine_select(out=ident[:], in_=ident[:], compare_op=ALU.not_equal, fill=1.0, base=0,
                                    pattern=[[-1, P]], channel_multiplier=1).then_inc(s_ident, 1)
            pool.wait_ge(d_nbd, 16)
            nc.gpsimd.tensor_copy(pbd[:].rearrange("p q a r -> p a q r"), nbd[:].rearrange("p a (q r) -> p a q r", r=RK)).then_inc(s_pbd, 1)
            pool.wait_ge(d_nb1, 16)
            nc.gpsimd.tensor_copy(pb1[:].rearrange("p q a r -> p a q r"), nb1[:].rearrange("p a (q r) -> p a q r", r=RK)).then_inc(s_pb1, 1)
            pool.wait_ge(s_zero, 3)
            pool.wait_ge(s_ident, 2)

            def low(dst, src, high, s):
                nc.gpsimd.tensor_tensor(dst, src, f(high), ALU.subtract).then_inc(s, 1)

            def ring_low(u, g):
                ring_loaded(pool, u, g)
                pool.wait_ge(s_rh[u], ring_count(u, g))
                src, h, l = ring_views(u)
                low(l, src, h, s_rl[u])

            def x_low(n):
                pool.wait_ge(s_xh, n + 1)
                low(xsl[:], xraw[:], xsh[:], s_xl)

            def w0_plus(n):
                pool.wait_ge(d_w0, 64 * (n + 1))
                seen(pool, s_w0l, n)
                nc.gpsimd.tensor_tensor(w0i[:], w0raw[:], ident[:], ALU.add).then_inc(s_w0i, 1)

            def w0_low(n):
                pool.wait_ge(s_w0i, n + 1)
                pool.wait_ge(s_w0h, n + 1)
                low(w0l[:], w0i[:], w0h[:], s_w0l)

            def gathered_low(dst, raw, s_high, s_low, n):
                pool.wait_ge(s_high, n + 1)
                high, lo = parts(dst)
                nc.gpsimd.tensor_tensor(lo, raw[:].rearrange("p b (k r) -> p k b r", r=RK), f(high),
                                        ALU.subtract).then_inc(s_low, 1)

            w0_plus(0)
            x_low(0)
            w0_low(0)
            gathered_low(ag1, ag1r, s_ag1h, s_ag1l, 0)
            ring_low("bg1", -1)
            gathered_low(agu, agur, s_aguh, s_agul, 0)

            def step(g, prev, nxt):
                ring_low("gate0", g)
                ring_low("up0", g)
                ring_low("gate1", g)
                ring_low("up1", g)
                if nxt:
                    w0_plus(g + 1)
                ring_low("gate2", g)
                if nxt:
                    w0_low(g + 1)
                    x_low(g + 1)
                ring_low("up2", g)
                if nxt:
                    gathered_low(ag1, ag1r, s_ag1h, s_ag1l, g + 1)
                gathered_low(agd, agdr, s_agdh, s_agdl, g)
                if nxt:
                    ring_low("bg1", g)
                    gathered_low(agu, agur, s_aguh, s_agul, g + 1)
                ring_low("bgd", g)

            loop(pool, step)

        @block.scalar
        def _(act):
            for dst, src in ((bci, c3), (bcc, chans), (bcs, seqlen)):
                act.dma_start(dst[:], src.partition_broadcast(P)).then_inc(d_tables, 16)
            halves = [slice(HID * half, HID * half + HID) for half in range(2)]
            for q in halves:
                act.dma_start(b3t[q, :], b3.rearrange("a h -> h a")).then_inc(d_tables, 16)
            act.wait_ge(s_zero, 3)
            for half, q in enumerate(halves):
                act.dma_start(w2raw[q, HID + CH * half:HID + CH * half + CH], W2).then_inc(d_small, 16)
            for b in range(NBG):
                act.dma_start(b2col[CH * b:CH * b + CH, :], b2.rearrange("(s o) -> s o", o=1)).then_inc(d_small, 16)
            act.wait_ge(d_nbu, 32)
            nc.scalar.copy(pbu[:].rearrange("p q a r -> p a q r"), nbu[:].rearrange("p a (q r) -> p a q r", r=RK)).then_inc(s_pbu, 1)
            act.wait_ge(d_small, 16 * 6)
            nc.scalar.copy(w2h[:], w2raw[:]).then_inc(s_w2h, 1)
            for u in range(11):
                act.wait_ge(s_ta, u + 1)
                src = bank[4 + u % 4]
                if u == 0:
                    last = nc.scalar.copy(tab1[:].rearrange("p a (k r) -> p k a r", r=RK),
                                          src[:].rearrange("p (k a r) -> p k a r", k=KH, r=RK))
                elif u < 5:
                    which, s = (u - 1) // 2, (u - 1) % 2
                    dst = tab2[:, 8 * s:8 * s + 8, which * KH * RK:(which + 1) * KH * RK]
                    last = nc.scalar.copy(dst.rearrange("p a (k r) -> p k a r", r=RK),
                                          src[:].rearrange("p (k a r) -> p k a r", k=KH, r=RK))
                else:
                    s, j = (u - 5) // 3, (u - 5) % 3
                    full = 4 if j < 2 else 2
                    c = 4 * j
                    dst = tab2[:, 8 * s:8 * s + 8, AGU + c * RK:AGU + (c + full) * RK]
                    last = nc.scalar.copy(dst.rearrange("p a (k r) -> p k a r", r=RK),
                                          src[:, 0:full * P].rearrange("p (k a r) -> p k a r", k=full, r=RK))
                    if j == 2:
                        c = FC - 1
                        last = nc.scalar.copy(tab2[0:FLAST, 8 * s:8 * s + 8, AGU + c * RK:AGU + (c + 1) * RK],
                                              src[0:FLAST, 2 * P:3 * P].rearrange("p (a r) -> p a r", r=RK))
                last.then_inc(s_ea, 1)

            def weights_high(units):
                for w in units:
                    act.wait_ge(s_tw, w + 1)
                    dst, src = weight_out(w, 0)
                    nc.scalar.copy(dst, src).then_inc(s_wh, 1)

            weights_high(range(WGU))

            def copy(dst, src, s):
                nc.scalar.activation(dst, src, ACT.Copy).then_inc(s, 1)

            def ring_high(u, g):
                ring_loaded(act, u, g)
                ring_free(act, u, g)
                src, h, _ = ring_views(u)
                copy(h, src, s_rh[u])

            def x_high(n):
                act.wait_ge(d_x, 16 * (n + 1))
                if isinstance(n, int) and n <= 1:
                    seen(act, s_l0, n)
                else:
                    act.wait_ge(s_h[1], n - 1)
                copy(xsh[:], xraw[:], s_xh)

            def w0_high(n):
                act.wait_ge(s_w0i, n + 1)
                seen(act, s_l0, n)
                copy(w0h[:], w0i[:], s_w0h)

            def gathered_high(dst, raw, d, used, s, n):
                act.wait_ge(d, 64 * (n + 1))
                seen(act, used, n)
                copy(parts(dst)[0], raw[:].rearrange("p b (k r) -> p k b r", r=RK), s)

            def stack_high(c, k, alone=False):
                act.wait_ge(s_tt[c], k + 1)
                stack_before(act, c, k, alone)
                n = ts[c].shape[1]
                copy(hh[:, 0:n], TURNED[c], s_hh[c])

            def x1_high(n):
                act.wait_ge(s_tx1, n + 1)
                copy(x1h, X[:], s_x1h)

            def x2_high(n):
                act.wait_ge(s_tx2, n + 1)
                copy(x2h[:], X[:], s_x2h)

            x_high(0)
            w0_high(0)
            x1_high(0)
            gathered_high(ag1, ag1r, d_ag1, s_l1a, s_ag1h, 0)
            ring_loaded(act, "bg1", -1)
            first_bg1, first_slot, _ = ring_views("bg1")
            copy(first_slot, first_bg1, s_rh["bg1"])
            stack_high("t1", 0)
            gathered_high(agu, agur, d_agu, s_ga, s_aguh, 0)
            x2_high(0)

            def silu(j, g):
                act.wait_ge(s_gate[j], g + 1)
                if j:
                    act.wait_ge(s_tr[j - 1], g + 1)
                else:
                    seen(act, s_tr[2], g)
                n = BLOCKS[j][1]
                nc.scalar.activation(sil[:, 0:n], GATE[j][:, 0:n], ACT.Silu).then_inc(s_sil[j], 1)

            def act_high(j, g):
                act.wait_ge(s_tr[j], g + 1)
                if j == 2:
                    act.wait_ge(s_dn[0], g + 1)
                else:
                    seen(act, s_dn[2 if j == 0 else 1], g)
                nf = -(-BLOCKS[j][1] // P) * P
                if j == 2:
                    nc.scalar.activation(ath[:, 0, 0:2 * P], TP[:, 0:2 * P], ACT.Copy)
                    copy(ath[0:FLAST, 0, 2 * P:3 * P], TP[0:FLAST, 2 * P:3 * P], s_ath[j])
                else:
                    copy(ath[:, j, 0:nf], TP[:, 0:nf], s_ath[j])

            def gelu(half, g):
                act.wait_ge(s_h[half], g + 1)
                seen(act, s_f3, g)
                nc.scalar.activation(graw[:, half, :], HB[half][:], ACT.Gelu,
                                     bias=cols[:, 3 + half:4 + half]).then_inc(s_gelu[half], 1)

            def gelu_high(half, g):
                act.wait_ge(s_gelu[half], g + 1)
                seen(act, s_o, g)
                copy(gh[:, half, :], graw[:, half, :], s_gh[half])

            def last_layer_a(g):
                gelu(0, g)
                gelu(1, g)
                gelu_high(0, g)
                gelu_high(1, g)

            def last_layer_b(g):
                act.wait_ge(s_o, g + 1)
                act.wait_ge(s_gl[0], g + 1)
                nc.scalar.activation(graw[:, 0, :], M[:], ACT.Identity, bias=b2col[:, 0:1]).then_inc(s_f1, 1)

            def w3_high(g):
                act.wait_ge(d_w3, 128 * (g + 1))
                act.wait_ge(s_meta, g + 1)
                seen(act, s_h[1], g)
                for half in range(2):
                    o = slice(half * P, half * P + P)
                    last = nc.scalar.activation(w3h[:, o], w3raw[:, o], ACT.Copy, scale=cols[:, half:half + 1])
                last.then_inc(s_w3h, 1)

            def x3_high(g, last):
                act.wait_ge(s_x3r, g + 1)
                act.wait_ge(s_l0, g + 1 if last else g + 2)
                nc.scalar.activation(x3s[0][0:SIDE], x3raw[0:SIDE, :], ACT.Copy)
                copy(x3s[1][SIDE:P], x3raw[SIDE:P, :], s_x3h)

            def step(g, prev, nxt):
                ring_high("gate0", g)
                stack_high("gu", g, not prev)
                ring_high("up0", g)
                if prev:
                    x3_high(g - 1, False)
                silu(0, g)
                ring_high("gate1", g)
                ring_high("up1", g)
                if prev:
                    last_layer_a(g - 1)
                ring_high("gate2", g)
                if not prev:
                    act.wait_ge(d_scr_b2, 32)
                    weights_high(DOWN_UNITS[0])
                    weights_high(DOWN_UNITS[1])
                if nxt:
                    w0_high(g + 1)
                    x_high(g + 1)
                if prev:
                    nc.scalar.activation(scrap[:], colf[:, 0:1], ACT.Silu)
                else:
                    weights_high(DOWN_UNITS[2])
                silu(1, g)
                ring_high("up2", g)
                if nxt:
                    gathered_high(ag1, ag1r, d_ag1, s_l1a, s_ag1h, g + 1)
                if not prev:
                    weights_high(DOWN_UNITS[3])
                act_high(0, g)
                if prev:
                    last_layer_b(g - 1)
                gathered_high(agd, agdr, d_agd, s_dn[2], s_agdh, g)
                silu(2, g)
                if nxt:
                    ring_high("bg1", g)
                    gathered_high(agu, agur, d_agu, s_ga, s_aguh, g + 1)
                act_high(1, g)
                if nxt:
                    x1_high(g + 1)
                ring_high("bgd", g)
                if nxt:
                    stack_high("t1", g + 1)
                act_high(2, g)
                if nxt:
                    x2_high(g + 1)
                w3_high(g)
                stack_high("td", g, not nxt)

            loop(act, step)
            nc.scalar.activation(scrap[:], colf[:, 0:1], ACT.Gelu)
            x3_high(G - 1, True)
            last_layer_a(G - 1)
            last_layer_b(G - 1)

        @block.vector
        def _(dve):
            chain = [0]

            def link(ins):
                chain[0] += 1
                ins.then_inc(s_chain, 1)
                dve.wait_ge(s_chain, chain[0])

            link(nc.vector.memset(tab2[FLAST:P, :, AGU + AGD - RK:AGU + AGD], 0.0))
            link(nc.vector.memset(mask[:], 0.0))
            for b in range(NBG):
                q = slice(CH * b, CH * b + CH)
                link(nc.vector.memset(mask[q, q], 1.0))
            dve.wait_ge(s_iota, 2)
            dve.wait_ge(s_ident, 2)
            link(nc.vector.tensor_scalar(pidx[:, 1:2], pidx[:, 0:1], CH - 1, None, ALU.bitwise_and))
            link(nc.vector.tensor_scalar(pidx[:, 2:3], pidx[:, 0:1], 4, 1, ALU.logical_shift_right, ALU.bitwise_and))
            link(nc.vector.tensor_copy(colf[:, 0:2], pidx[:, 1:3]))
            link(nc.vector.tensor_scalar(colf[:, 2:3], colf[:, 1:2], -2.0, 1.0, ALU.mult, ALU.add))
            dve.wait_ge(d_nbg, 32)
            nc.vector.tensor_copy(pbg[:].rearrange("p q a r -> p a q r"), nbg[:].rearrange("p a (q r) -> p a q r", r=RK)).then_inc(s_pbg, 1)

            def rank_rows(u):
                dve.wait_ge(s_tb, u + 1)
                src = bank[u % 4]
                if u < 16:
                    t, s, q = u // 8, (u // 4) % 2, u % 4
                    dst = rows2[:, s, t * F:(t + 1) * F].rearrange("p (m q i) -> p q i m", q=4, i=4)[:, q]
                    last = nc.vector.tensor_copy(dst, src[:, 0:4 * FP].rearrange("p (i m) -> p i m", i=4))
                elif u < 18:
                    dst = rows2[:, u - 16, 2 * F:BROW].rearrange("p (m i) -> p i m", i=KH)
                    last = nc.vector.tensor_copy(dst, src[:].rearrange("p (i m) -> p i m", i=KH))
                else:
                    last = nc.vector.tensor_copy(rows1[:].rearrange("p (m i) -> p i m", i=KH),
                                                 src[:].rearrange("p (i m) -> p i m", i=KH))
                last.then_inc(s_eb, 1)

            for u in range(8):
                rank_rows(u)
            dve.wait_ge(d_tables, 16 * 5)
            for b in range(NBG):
                q = slice(CH * b, CH * b + CH)
                for half in range(2):
                    link(nc.vector.tensor_scalar(meta[q, :, half], bcc[q, :].rearrange("p (g b) -> p b g", b=NBG)[:, 2 * half + b % 2],
                                                 colf[q, 0:1], None, ALU.is_gt))
                link(nc.vector.tensor_copy(meta[q, :, 2], bcs[q, :].rearrange("p (g b) -> p b g", b=NBG)[:, b]))
            for half in range(2):
                q = slice(HID * half, HID * half + HID)
                link(nc.vector.tensor_copy(pair[q], bci[q, :].rearrange("p (g s b) -> p g s b", s=2, b=2)[:, :, :, half]))
            for a in range(NS):
                dst = btmp[:] if a else meta[:, :, 3:5]
                link(nc.vector.tensor_scalar(dst, pair[:], float(a), b3t[:, a:a + 1], ALU.is_equal, ALU.mult))
                if a:
                    link(nc.vector.tensor_tensor(meta[:, :, 3:5], meta[:, :, 3:5], btmp[:], ALU.add))
            nc.vector.tensor_copy(cols[:], meta[:, 0, :]).then_inc(s_const, 1)
            for u in range(8, 19):
                rank_rows(u)
            dve.wait_ge(s_w2h, 1)
            link(nc.vector.tensor_tensor(w2l[:], w2raw[:], f(w2h[:]), ALU.subtract))

            def weights_low(units):
                for w in units:
                    dve.wait_ge(s_wh, w + 1)
                    dst, src = weight_out(w, 1)
                    high, _ = weight_out(w, 0)
                    nc.vector.tensor_tensor(dst, src, f(high), ALU.subtract).then_inc(s_wl, 1)

            weights_low(range(WGU))

            def low(dst, src, high, s):
                nc.vector.tensor_tensor(dst, src, f(high), ALU.subtract).then_inc(s, 1)

            def add_parts(c, scale, k, product, before, count, free, times):
                dve.wait_ge(product, k + 1)
                seen(dve, s_sum[before], count)
                n = ts[c].shape[1]
                w = n // P
                nc.vector.scalar_tensor_tensor(
                    out=tm[:, 0:n].rearrange("p (w n) -> p w n", w=w), in0=COEF[c].rearrange("p (w n) -> p w n", w=w),
                    scalar=scale, in1=mask[:].unsqueeze(1).broadcast_to([P, w, P]),
                    op0=ALU.mult, op1=ALU.mult).then_inc(s_tm[c], 1)
                dve.wait_ge(s_tm[c], k + 1)
                seen(dve, s_tt[free], times)
                v = tm[:, 0:n].rearrange("p (b c r) -> p b c r", c=2, r=RK)
                q = [v[:, :, i:i + 1, :].broadcast_to([P, w * NBG, 2, RK]) for i in range(2)]
                nc.vector.tensor_tensor(tsum[c][:].rearrange("p (b c r) -> p b c r", c=2, r=RK), q[0], q[1],
                                        ALU.add).then_inc(s_sum[c], 1)

            def stack(c, k, alone=False):
                dve.wait_ge(s_hh[c], k + 1)
                stack_before(dve, c, k, alone)
                n = ts[c].shape[1]
                nc.vector.tensor_scalar(tms[:, 0:n], TURNED[c], colf[:, 1:2], None, ALU.mult).then_inc(s_tms[c], 1)
                dve.wait_ge(s_tms[c], k + 1)
                nc.vector.scalar_tensor_tensor(out=ts[c][:], in0=f(hh[:, 0:n]), scalar=colf[:, 2:3], in1=tms[:, 0:n],
                                               op0=ALU.mult, op1=ALU.add).then_inc(s_ts[c], 1)

            def add_t1(n):
                add_parts("t1", 1.0, n, s_l1a, "gu", n, "td", max(n - 1, 0) if isinstance(n, int) else n - 1)

            def stack_t1(n):
                if not (isinstance(n, int) and n < 2):
                    dve.wait_ge(s_x3, n - 1)
                stack("t1", n)

            def add_td(g, last):
                if last:
                    add_parts("td", 0.5, g, s_dn[2], "gu", g + 1, "td", g)
                else:
                    add_parts("td", 0.5, g, s_dn[2], "t1", g + 2, "t1", g + 2)

            def stack_td(g, last):
                dve.wait_ge(s_l1b, g + 1 if last else g + 2)
                stack("td", g, last)

            def add_gu(n, first):
                add_parts("gu", 0.5, n, s_ga, "t1" if first else "td", 1 if first else n, "gu", n)

            def stack_gu(n, first):
                seen(dve, s_up[2], n)
                stack("gu", n, first)

            def x1_row(n):
                dve.wait_ge(s_l0, n + 1)
                if not (isinstance(n, int) and n < 2):
                    dve.wait_ge(s_f3, n - 1)
                nc.vector.tensor_copy(x1row, R[:]).then_inc(s_x1r, 1)

            def x1_low(n):
                dve.wait_ge(s_x1h, n + 1)
                low(x1l, X[:], x1h, s_x1l)

            def x2_row(n):
                dve.wait_ge(s_l1b, n + 1)
                seen(dve, s_pre, n)
                nc.vector.tensor_copy(x2row[:], R[:]).then_inc(s_x2r, 1)

            def x2_low(n):
                dve.wait_ge(s_x2h, n + 1)
                low(x2l[:], X[:], x2h[:], s_x2l)

            def keep_x2(g):
                seen(dve, d_out, g * 16)
                nc.vector.tensor_copy(x3raw[:], x2row[:]).then_inc(s_pre, 1)

            x1_row(0)
            x1_low(0)
            add_t1(0)
            stack_t1(0)
            x2_row(0)
            x2_low(0)
            add_gu(0, True)

            def mul(j, g):
                dve.wait_ge(s_sil[j], g + 1)
                dve.wait_ge(s_up[j], g + 1)
                n = BLOCKS[j][1]
                nc.vector.tensor_tensor(sil[:, 0:n], UP[j][:, 0:n], sil[:, 0:n], ALU.mult).then_inc(s_mul[j], 1)

            def act_low(j, g):
                dve.wait_ge(s_ath[j], g + 1)
                if j == 2:
                    nc.vector.tensor_tensor(atl[:, 0, 0:2 * P], TP[:, 0:2 * P], f(ath[:, 0, 0:2 * P]), ALU.subtract)
                    low(atl[0:FLAST, 0, 2 * P:3 * P], TP[0:FLAST, 2 * P:3 * P], ath[0:FLAST, 0, 2 * P:3 * P], s_atl[j])
                else:
                    low(atl[:, j, :], TP[:], ath[:, j, :], s_atl[j])

            def gelu_low(g):
                for half in range(2):
                    dve.wait_ge(s_gh[half], g + 1)
                    low(gl[:, half, :], graw[:, half, :], gh[:, half, :], s_gl[half])

            def finish(g):
                dve.wait_ge(s_f1, g + 1)
                nc.vector.scalar_tensor_tensor(out=graw[:, 1, :], in0=iota_t[:], scalar=cols[:, 2:3], in1=graw[:, 0, :],
                                               op0=ALU.is_lt, op1=ALU.mult).then_inc(s_f2, 1)
                dve.wait_ge(s_f2, g + 1)
                nc.vector.tensor_tensor(x3raw[:], x3raw[:], graw[:, 1, :], ALU.add).then_inc(s_f3, 1)

            def next_cols(g):
                if isinstance(g, int) and g == 0:
                    dve.wait_ge(s_const, 1)
                nc.vector.tensor_copy(cols[:], meta[:, bass.ds(g, 1), :].rearrange("p g c -> p (g c)")).then_inc(s_meta, 1)

            def x3_row(g):
                dve.wait_ge(s_x3, g + 1)
                dve.wait_ge(s_pre, g + 1)
                nc.vector.tensor_tensor(x3raw[:, 0:HALF], D[:, 0:HALF], x3raw[:, 0:HALF], ALU.add)
                nc.vector.tensor_tensor(x3raw[:, HALF:T], M[:, 0:HALF], x3raw[:, HALF:T], ALU.add).then_inc(s_x3r, 1)
                dve.wait_ge(s_x3h, g + 1)
                nc.vector.tensor_tensor(x3s[0][SIDE:P], x3raw[0:SIDE, :], f(x3s[0][0:SIDE]), ALU.subtract)
                low(x3s[1][0:SIDE], x3raw[SIDE:P, :], x3s[1][SIDE:P], s_x3l)

            def step(g, prev, nxt):
                stack_gu(g, not prev)
                if prev:
                    x3_row(g - 1)
                mul(0, g)
                if prev:
                    gelu_low(g - 1)
                else:
                    for lot in DOWN_UNITS[0:3]:
                        weights_low(lot)
                mul(1, g)
                if not prev:
                    weights_low(DOWN_UNITS[3])
                act_low(0, g)
                if prev:
                    finish(g - 1)
                next_cols(g)
                if nxt:
                    x1_row(g + 1)
                mul(2, g)
                act_low(1, g)
                if nxt:
                    x1_low(g + 1)
                    add_t1(g + 1)
                    stack_t1(g + 1)
                act_low(2, g)
                keep_x2(g)
                if nxt:
                    x2_row(g + 1)
                    x2_low(g + 1)
                dve.wait_ge(s_w3h, g + 1)
                for half in range(2):
                    o = slice(half * P, half * P + P)
                    last = nc.vector.scalar_tensor_tensor(out=w3l[:, o], in0=w3raw[:, o], scalar=cols[:, half:half + 1],
                                                          in1=f(w3h[:, o]), op0=ALU.mult, op1=ALU.subtract)
                last.then_inc(s_w3l, 1)
                add_td(g, not nxt)
                if nxt:
                    add_gu(g + 1, False)
                stack_td(g, not nxt)

            loop(dve, step)
            x3_row(G - 1)
            gelu_low(G - 1)
            finish(G - 1)

        @block.tensor
        def _(pe):
            pe.wait_ge(s_ident, 2)

            def tr(dst, src, n):
                return nc.tensor.transpose(dst, src, ident[0:n, 0:n])

            def b_unit(u):
                for first, ready in ((0, s_pbg), (8, s_pbu), (16, s_pbd), (18, s_pb1)):
                    if u == first:
                        pe.wait_ge(ready, 1)
                if u >= 4:
                    pe.wait_ge(s_eb, u - 3)
                dst = bank[u % 4]
                for i in range(4):
                    if u < 16:
                        t, s, q = u // 8, (u // 4) % 2, u % 4
                        src = (pbg, pbu)[t][:, 4 * q + i, 8 * s:8 * s + 8, :].rearrange("p a r -> p (a r)")
                        last = tr(dst[:, i * FP:(i + 1) * FP], src, FP)
                    else:
                        src = pbd[:, i, 8 * (u - 16):8 * (u - 16) + 8, :] if u < 18 else pb1[:, i]
                        last = tr(dst[:, i * P:(i + 1) * P], src.rearrange("p a r -> p (a r)"), P)
                last.then_inc(s_tb, 1)

            def a_unit(u):
                if u == 0:
                    pe.wait_ge(d_an, 64)
                if u >= 4:
                    pe.wait_ge(s_ea, u - 3)
                dst = bank[4 + u % 4]
                if u == 0:
                    pieces = [(na1[:, k * P:(k + 1) * P], P) for k in range(KH)]
                elif u < 5:
                    which, s = (u - 1) // 2, (u - 1) % 2
                    pieces = [((nag, nau)[which][:, s, k * P:(k + 1) * P], P) for k in range(KH)]
                else:
                    s, j = (u - 5) // 3, (u - 5) % 3
                    pieces = [(nad[:, s, c * P:min(F, (c + 1) * P)], min(P, F - c * P)) for c in range(4 * j, min(FC, 4 * j + 4))]
                for i, (src, m) in enumerate(pieces):
                    last = tr(dst[0:m, i * P:(i + 1) * P], src, P)
                last.then_inc(s_ta, 1)

            for u in range(19):
                b_unit(u)
                if u >= 8:
                    a_unit(u - 8)
            pe.wait_ge(s_ea, 11)
            pe.wait_ge(s_eb, 19)

            def weight_units(units, busy):
                for w in units:
                    if w - busy >= (0 if w < WGU else WGU):
                        pe.wait_ge(s_wl, w - busy + 1)
                    dst = weight_bank(w)
                    if w < WGU:
                        t, k, j = w // 12, (w % 12) // 3, w % 3
                        for c in range(4 * j, min(FC, 4 * j + 4)):
                            m = min(P, F - c * P)
                            o = (c - 4 * j) * P
                            last = tr(dst[:, o:o + m], (nwg, nwu)[t][0:m, c, k * P:(k + 1) * P], m)
                    else:
                        c = w - WGU
                        m = min(P, F - c * P)
                        for k in range(KH):
                            last = tr(dst[0:m, k * P:(k + 1) * P], nwd[:, k, c * P:c * P + m], P)
                    last.then_inc(s_tw, 1)

            pe.wait_ge(d_nwg, 32)
            weight_units(range(WGU // 2), 8)
            pe.wait_ge(d_nwu, 32)
            weight_units(range(WGU // 2, WGU), 8)
            pe.wait_ge(s_wl, WGU)

            def passes(dst, sh, sl, mh, ml, first, last_):
                nc.tensor.matmul(dst, sh, mh, start=first, stop=False)
                nc.tensor.matmul(dst, sl, mh, start=False, stop=False)
                return nc.tensor.matmul(dst, sh, ml, start=False, stop=last_)

            def turn(c, k):
                pe.wait_ge(s_sum[c], k + 1)
                for i in range(ts[c].shape[1] // P):
                    last = tr(TURNED[c][:, i * P:(i + 1) * P], tsum[c][:, i * P:(i + 1) * P], P)
                last.then_inc(s_tt[c], 1)

            def chunk(ap, k):
                return ap[:, k * P:(k + 1) * P]

            def layer0(n):
                pe.wait_ge(s_xl, n + 1)
                pe.wait_ge(s_w0l, n + 1)
                seen(pe, s_mul[1], n)
                passes(R[:], w0h[:], w0l[:], xsh[:], xsl[:], True, True).then_inc(s_l0, 1)

            def turn_x(src, ready, done, n):
                pe.wait_ge(ready, n + 1)
                for k in range(KH):
                    last = tr(chunk(X, k), chunk(src, k), P)
                last.then_inc(done, 1)

            def turn_x1(n):
                seen(pe, s_x2l, n)
                turn_x(x1row, s_x1r, s_tx1, n)

            def turn_x2(n):
                turn_x(x2row, s_x2r, s_tx2, n)

            def layer1_a(n):
                pe.wait_ge(s_x1l, n + 1)
                pe.wait_ge(s_ag1l, n + 1)
                for k in range(KH):
                    nc.tensor.matmul(COEF["t1"], chunk(x1h, k), ag1[:, k, :], start=(k == 0), stop=False)
                    last = nc.tensor.matmul(COEF["t1"], chunk(x1l, k), ag1[:, k, :], start=False, stop=(k == KH - 1))
                last.then_inc(s_l1a, 1)

            def rank_b(dst, stat, u, n, o=0, check=True):
                i = RING.index(u) % 2
                nc.tensor.matmul(dst, stat, ringh[:, i, o:o + n], start=False, stop=False, skip_group_check=not check)
                return nc.tensor.matmul(dst, stat, ringl[:, i, o:o + n], start=False, stop=True, skip_group_check=not check)

            def layer1_b(n):
                pe.wait_ge(s_ts["t1"], n + 1)
                pe.wait_ge(s_rl["bg1"], n + 1)
                rank_b(R[:], ts_x[:], "bg1", T, check=False).then_inc(s_l1b, 1)

            def rank_gu_a(n):
                pe.wait_ge(s_x2l, n + 1)
                pe.wait_ge(s_agul, n + 1)
                for k in range(KH):
                    both = agu[:].rearrange("p (w k) n -> p k w n", w=2)[:, k]
                    nc.tensor.matmul(COEF["gu"], chunk(x2h, k), both, start=(k == 0), stop=False)
                    last = nc.tensor.matmul(COEF["gu"], chunk(x2l, k), both, start=False, stop=(k == KH - 1))
                last.then_inc(s_ga, 1)

            def dense(which, j, chunks=range(KH)):
                f0, n = BLOCKS[j]
                dst, o = (GATE, UP)[which][j], which * F + f0
                for k in chunks:
                    passes(dst[:, 0:n], chunk(x2h, k), chunk(x2l, k), wguh[:, k, o:o + n], wgul[:, k, o:o + n],
                           k == 0, False)

            def rank_gu_b(which, j, g):
                n = BLOCKS[j][1]
                pe.wait_ge(s_ts["gu"], g + 1)
                u = ("gate", "up")[which] + str(j)
                pe.wait_ge(s_rl[u], g + 1)
                rank_b((GATE, UP)[which][j][:, 0:n], ts_gu[:, which * P:(which + 1) * P], u, n) \
                    .then_inc((s_gate, s_up)[which][j], 1)

            def transpose_act(j, g):
                pe.wait_ge(s_mul[j], g + 1)
                if j:
                    pe.wait_ge(s_atl[j - 1], g + 1)
                else:
                    seen(pe, s_gelu[1], g)
                for i in range(-(-BLOCKS[j][1] // P)):
                    m = min(P, BLOCKS[j][1] - i * P)
                    last = tr(TP[0:m, i * P:(i + 1) * P], sil[:, i * P:i * P + m], P)
                last.then_inc(s_tr[j], 1)

            def down(c, g):
                j, i = c // 4, c % 4
                if c == 0:
                    pe.wait_ge(s_agdl, g + 1)
                    seen(pe, s_gelu[0], g)
                    seen(pe, s_f1, g)
                if i == 0:
                    pe.wait_ge(s_atl[j], g + 1)
                m = min(P, F - c * P)
                h, l = (a[0:m, j % 2, i * P:(i + 1) * P] for a in (ath, atl))
                end = c == FC - 1
                first = c == 0
                if end:
                    nc.tensor.matmul(M[:, 0:HALF], h, wdl[0:m, c, HALF:T], start=False, stop=False, skip_group_check=True)
                nc.tensor.matmul(D[:, 0:HALF], h, wdh[0:m, c, 0:HALF], start=first, stop=False)
                nc.tensor.matmul(M[:, 0:HALF + P], h, wdh[0:m, c, HALF:T + P], start=first, stop=False)
                nc.tensor.matmul(D[:, 0:HALF], h, wdl[0:m, c, 0:HALF], start=False, stop=False)
                if not end:
                    nc.tensor.matmul(M[:, 0:HALF], h, wdl[0:m, c, HALF:T], start=False, stop=False)
                nc.tensor.matmul(D[:, 0:HALF], l, wdh[0:m, c, 0:HALF], start=False, stop=end)
                last = nc.tensor.matmul(M[:, 0:HALF + P], l, wdh[0:m, c, HALF:T + P], start=False, stop=end)
                if i == 3 or end:
                    last.then_inc(s_dn[j], 1)

            def rank_down_b(g):
                pe.wait_ge(s_ts["td"], g + 1)
                pe.wait_ge(s_rl["bgd"], g + 1)
                rank_b(D[:, 0:HALF], ts_x[:], "bgd", HALF, 0, check=False)
                rank_b(M[:, 0:HALF], ts_x[:], "bgd", HALF, HALF, check=False).then_inc(s_x3, 1)

            def layer3_a(g):
                pe.wait_ge(s_x3l, g + 1)
                pe.wait_ge(s_w3l, g + 1)
                for half in range(2):
                    nc.tensor.matmul(HB[half][:], chunk(w3h, half), x3s[half][:], start=True, stop=False)
                    nc.tensor.matmul(HB[half][:], chunk(w3l, half), x3s[half][:], start=False, stop=True).then_inc(s_h[half], 1)

            def layer3_b(g):
                for half in range(2):
                    pe.wait_ge(s_gl[half], g + 1)
                    o = HID * (1 - half)
                    last = passes(M[:], w2h[:, o:o + P], w2l[:, o:o + P], gh[:, half, :], gl[:, half, :], half == 0, half == 1)
                last.then_inc(s_o, 1)

            layer0(0)
            turn_x1(0)
            layer1_a(0)
            turn("t1", 0)
            layer1_b(0)
            turn_x2(0)
            rank_gu_a(0)

            def step(g, prev, nxt):
                seen(pe, s_mul[2], g)
                dense(0, 0)
                turn("gu", g)
                if prev:
                    rank_down_b(g - 1)
                dense(1, 0)
                rank_gu_b(0, 0, g)
                rank_gu_b(1, 0, g)
                dense(0, 1, range(0, 2))
                if prev:
                    layer3_a(g - 1)
                dense(0, 1, range(2, KH))
                rank_gu_b(0, 1, g)
                if not prev:
                    pe.wait_ge(d_nwd, 16)
                    weight_units(DOWN_UNITS[0], 3)
                dense(1, 1, range(0, 2))
                if not prev:
                    weight_units(DOWN_UNITS[1], 3)
                dense(1, 1, range(2, KH))
                rank_gu_b(1, 1, g)
                if not prev:
                    weight_units(DOWN_UNITS[2], 3)
                transpose_act(0, g)
                if prev:
                    layer3_b(g - 1)
                else:
                    weight_units(DOWN_UNITS[3], 3)
                pe.wait_ge(s_mul[0], g + 1)
                dense(0, 2)
                rank_gu_b(0, 2, g)
                if nxt:
                    layer0(g + 1)
                transpose_act(1, g)
                dense(1, 2)
                rank_gu_b(1, 2, g)
                if not prev:
                    pe.wait_ge(s_wl, WALL)
                if nxt:
                    turn_x1(g + 1)
                for c in range(FC):
                    down(c, g)
                    if c == 2 and nxt:
                        layer1_a(g + 1)
                    if c == 3 and nxt:
                        turn("t1", g + 1)
                    if c == 3:
                        transpose_act(2, g)
                    if c == 5 and nxt:
                        layer1_b(g + 1)
                    if c == 7 and nxt:
                        turn_x2(g + 1)
                if nxt:
                    rank_gu_a(g + 1)
                turn("td", g)

            loop(pe, step)
            rank_down_b(G - 1)
            layer3_a(G - 1)
            layer3_b(G - 1)


_INS = ["x", "itok_B_0_15", "itok_B_3_7", "itok_B_2_6", "itok_B_0_7", "itok_B_2182_4065", "_lenS",
        "L0_cond_weights", "L1_cond_A", "L1_cond_B", "L2_cond_W_gate", "L2_cond_W_up", "L2_cond_W_down",
        "L2_cond_A_gate", "L2_cond_B_gate", "L2_cond_A_up", "L2_cond_B_up", "L2_cond_A_down",
        "L2_cond_B_down", "L3_cond_W_sess", "L3_cond_b_sess", "L3_cond_W2", "L3_cond_b2"]


def kernel(**inputs):
    import numpy as _np
    import concourse.bass as _bass
    import concourse.bacc as _bacc
    from concourse import mybir as _mybir
    from concourse.bass_utils import run_bass_kernel_spmd as _run

    nc = _bacc.Bacc("TRN2", target_bir_lowering=False, num_devices=1, dynamic_dma_scratch_size=1024)
    arrays, args = {}, []
    for name in _INS:
        a = _np.ascontiguousarray(inputs[name])
        arrays[f"in_{name}_dram"] = a
        args.append(nc.dram_tensor(f"in_{name}_dram", a.shape, _mybir.dt.from_np(a.dtype), kind="ExternalInput").ap())
    out = nc.dram_tensor("out_0_dram", (BATCH, CH, T), _mybir.dt.float32, kind="ExternalOutput").ap()
    build(nc, _bass, _mybir, *args, out)
    r = _run(nc, [arrays], core_ids=[0])
    return r.results[0]["out_0_dram"]
```
